# Optimizing a Trainium2 kernel written in Bass

```python
import numpy as np
import jax
import jax.numpy as jnp

def _softmax(x, axis=-1):
    return jax.nn.softmax(x, axis=axis)

def _gelu(x):
    return jax.nn.gelu(x, approximate=True)

def _silu(x):
    return jax.nn.silu(x)

def _sigmoid(x):
    return jax.nn.sigmoid(x)

def _layernorm(x, axis=-1, eps=1e-05):
    m = jnp.mean(x, axis=axis, keepdims=True)
    v = jnp.var(x, axis=axis, keepdims=True)
    return (x - m) / jnp.sqrt(v + eps)

def _scatter_add(tgt, idx, src, axis=0):
    return tgt.at[idx].add(src)

def _segment_sum(src, seg, n):
    return jax.ops.segment_sum(src, seg, n)
kernel_name = 'mk_pixart_seq_d4_seqx_r4_9c30e6'

def setup_inputs(seed: int=0):
    np.random.seed(seed)
    _w = jnp.asarray

    def _rec_inputs():
        import jax
        import jax.numpy as jnp
        _rk = jax.random.key(seed)
        x = -0.0005207 + 1.001 * jax.random.normal(jax.random.fold_in(_rk, 1), (8, 256, 256), jnp.float32)
        _lenS = 256 - jax.random.randint(jax.random.fold_in(_rk, 7), (8,), 0, max(1, 256 // 4) + 1, jnp.int32)
        _lenS2 = 77 - jax.random.randint(jax.random.fold_in(_rk, 8), (8,), 0, max(1, 77 // 4) + 1, jnp.int32)
        cond_1024 = 0.000887014 + 1.03683 * jax.random.normal(jax.random.fold_in(_rk, 11), (8, 256), jnp.float32)
        _ctx_768P = jax.random.normal(jax.random.fold_in(_rk, 12), (8, 16, 192), jnp.float32)
        _ctx_768c = jax.random.dirichlet(jax.random.fold_in(_rk, 512), 0.3 * jnp.ones((16,), jnp.float32), (8, 77))
        _ctx_768t = jnp.einsum('bsk,bkd->bsd', _ctx_768c, _ctx_768P)
        _ctx_768t = _ctx_768t * jax.lax.rsqrt(jnp.mean(jnp.square(_ctx_768t)) + 1e-12) * 0.953939
        ctx_768 = 0.000599585 + 1.00006 * (_ctx_768t + 0.3 * jax.random.normal(jax.random.fold_in(_rk, 612), (8, 77, 192), jnp.float32))
        return (x, cond_1024, ctx_768)
    x, cond_1024, ctx_768 = _rec_inputs()

    def _L0_xcond_setup():
        import jax, jax.numpy as jnp
        import numpy as np
        B, N, M = (2, 256, 128)
        D, H, DH = (256, 16, 64)
        MID = H * DH
        DC = 192
        MULT = 4
        EPS = 1e-05

        def _ln(x, w, b):
            mu = jnp.mean(x, -1, keepdims=True)
            var = jnp.mean((x - mu) ** 2, -1, keepdims=True)
            return (x - mu) * jax.lax.rsqrt(var + EPS) * w + b

        def _sincos(n, d):
            inv = 1.0 / 10000.0 ** (jnp.arange(0, d, 2, dtype=jnp.float32) / d)
            ang = jnp.arange(n, dtype=jnp.float32)[:, None] * inv[None, :]
            return (jnp.sin(ang), jnp.cos(ang))

        def _rope(x, sin, cos):
            s = sin[None, None]
            c = cos[None, None]
            xe = x[..., ::2]
            xo = x[..., 1::2]
            re = xe * c - xo * s
            ro = xe * s + xo * c
            return jnp.stack((re, ro), axis=-1).reshape(x.shape)

        def _heads(t):
            b, n, _ = t.shape
            return t.reshape(b, n, H, DH).transpose(0, 2, 1, 3)

        def _attn(xq, ctx, wq, wkv, wo, bo):
            q = _heads(xq @ wq)
            k, v = jnp.split(ctx @ wkv, 2, axis=-1)
            k = _heads(k)
            v = _heads(v)
            sq, cq = _sincos(q.shape[2], DH)
            sk, ck = _sincos(k.shape[2], DH)
            q = _rope(q, sq, cq)
            k = _rope(k, sk, ck)
            sim = jnp.einsum('bhnd,bhmd->bhnm', q, k) * DH ** (-0.5)
            a = jax.nn.softmax(sim, axis=-1)
            o = jnp.einsum('bhnm,bhmd->bhnd', a, v)
            o = o.transpose(0, 2, 1, 3).reshape(xq.shape[0], xq.shape[1], MID)
            return o @ wo + bo

        def _adaln(x, c, lw, lb, gw, gb, bw, bb):
            g = (c @ gw + gb)[:, None, :]
            bt = (c @ bw + bb)[:, None, :]
            return _ln(x, lw, lb) * (1.0 + g) + bt
        ks = jax.random.split(jax.random.key(seed), 24)
        s = 0.02
        inp = {'x': jax.random.normal(ks[0], (B, N, D), jnp.float32), 'cond': jax.random.normal(ks[1], (B, D), jnp.float32), 'context': jax.random.normal(ks[2], (B, M, DC), jnp.float32), 'ln1_w': jnp.ones((D,), jnp.float32), 'ln1_b': jnp.zeros((D,), jnp.float32), 'g1_w': jax.random.normal(ks[3], (D, D), jnp.float32) * s, 'g1_b': jnp.zeros((D,), jnp.float32), 'b1_w': jax.random.normal(ks[4], (D, D), jnp.float32) * s, 'b1_b': jnp.zeros((D,), jnp.float32), 'ln2_w': jnp.ones((D,), jnp.float32), 'ln2_b': jnp.zeros((D,), jnp.float32), 'g2_w': jax.random.normal(ks[5], (D, D), jnp.float32) * s, 'g2_b': jnp.zeros((D,), jnp.float32), 'b2_w': jax.random.normal(ks[6], (D, D), jnp.float32) * s, 'b2_b': jnp.zeros((D,), jnp.float32), 'sa_wq': jax.random.normal(ks[7], (D, MID), jnp.float32) * s, 'sa_wkv': jax.random.normal(ks[8], (D, 2 * MID), jnp.float32) * s, 'sa_wo': jax.random.normal(ks[9], (MID, D), jnp.float32) * s, 'sa_bo': jnp.zeros((D,), jnp.float32), 'ca_lnc_w': jnp.ones((DC,), jnp.float32), 'ca_lnc_b': jnp.zeros((DC,), jnp.float32), 'ca_wq': jax.random.normal(ks[10], (D, MID), jnp.float32) * s, 'ca_wkv': jax.random.normal(ks[11], (DC, 2 * MID), jnp.float32) * s, 'ca_wo': jax.random.normal(ks[12], (MID, D), jnp.float32) * s, 'ca_bo': jnp.zeros((D,), jnp.float32), 'ff_w1': jax.random.normal(ks[13], (D, MULT * D), jnp.float32) * s, 'ff_b1': jnp.zeros((MULT * D,), jnp.float32), 'ff_w2': jax.random.normal(ks[14], (MULT * D, D), jnp.float32) * s, 'ff_b2': jnp.zeros((D,), jnp.float32)}
        return inp
    _L0_xcond_all = _L0_xcond_setup()
    _L0_xcond_in = {k: v for k, v in _L0_xcond_all.items() if k in ('ln1_w', 'ln1_b', 'g1_w', 'g1_b', 'b1_w', 'b1_b', 'ln2_w', 'ln2_b', 'g2_w', 'g2_b', 'b2_w', 'b2_b', 'sa_wq', 'sa_wkv', 'sa_wo', 'sa_bo', 'ca_lnc_w', 'ca_lnc_b', 'ca_wq', 'ca_wkv', 'ca_wo', 'ca_bo', 'ff_w1', 'ff_b1', 'ff_w2', 'ff_b2')}
    del _L0_xcond_all

    def _L1_xcond_setup():
        import jax, jax.numpy as jnp
        import numpy as np
        EPS = 1e-05

        def _ada_ln(x, t, W, b):
            emb = t @ W + b
            scale, shift = jnp.split(emb, 2, axis=-1)
            mu = x.mean(-1, keepdims=True)
            var = ((x - mu) ** 2).mean(-1, keepdims=True)
            xn = (x - mu) * jax.lax.rsqrt(var + EPS)
            return xn * (1.0 + scale) + shift

        def _attn(x, ctx, Wq, Wk, Wv, Wo, bo, heads):
            b, n, _ = x.shape
            j = ctx.shape[1]
            q = (x @ Wq).reshape(b, n, heads, -1)
            k = (ctx @ Wk).reshape(b, j, heads, -1)
            v = (ctx @ Wv).reshape(b, j, heads, -1)
            scale = q.shape[-1] ** (-0.5)
            sim = jnp.einsum('bihd,bjhd->bhij', q, k) * scale
            attn = jax.nn.softmax(sim, axis=-1)
            out = jnp.einsum('bhij,bjhd->bihd', attn, v).reshape(b, n, -1)
            return out @ Wo + bo

        def _ff(x, W1, b1, W2, b2):
            p = x @ W1 + b1
            a, gate = jnp.split(p, 2, axis=-1)
            return a * jax.nn.gelu(gate, approximate=False) @ W2 + b2
        key = jax.random.key(seed)
        ks = jax.random.split(key, 32)
        B, N, D = (4, 512, 256)
        J, CD = (64, 192)
        H, DH = (16, 64)
        INNER = H * DH
        FF = 4 * D
        w = lambda k, shp: jax.random.normal(k, shp, jnp.float32) * 0.02
        inp = {'x': jax.random.normal(ks[0], (B, N, D), jnp.float32), 't': jax.random.normal(ks[1], (B, 1, D), jnp.float32), 'context': jax.random.normal(ks[2], (B, J, CD), jnp.float32), 'n1_w': w(ks[3], (D, 2 * D)), 'n1_b': jnp.zeros((2 * D,), jnp.float32), 'n2_w': w(ks[4], (D, 2 * D)), 'n2_b': jnp.zeros((2 * D,), jnp.float32), 'n3_w': w(ks[5], (D, 2 * D)), 'n3_b': jnp.zeros((2 * D,), jnp.float32), 'q1': w(ks[6], (D, INNER)), 'k1': w(ks[7], (D, INNER)), 'v1': w(ks[8], (D, INNER)), 'o1_w': w(ks[9], (INNER, D)), 'o1_b': jnp.zeros((D,), jnp.float32), 'q2': w(ks[10], (D, INNER)), 'k2': w(ks[11], (CD, INNER)), 'v2': w(ks[12], (CD, INNER)), 'o2_w': w(ks[13], (INNER, D)), 'o2_b': jnp.zeros((D,), jnp.float32), 'ff_w1': w(ks[14], (D, 2 * FF)), 'ff_b1': jnp.zeros((2 * FF,), jnp.float32), 'ff_w2': w(ks[15], (FF, D)), 'ff_b2': jnp.zeros((D,), jnp.float32)}
        return inp
    _L1_xcond_all = _L1_xcond_setup()
    _L1_xcond_in = {k: v for k, v in _L1_xcond_all.items() if k in ('n1_w', 'n1_b', 'n2_w', 'n2_b', 'n3_w', 'n3_b', 'q1', 'k1', 'v1', 'o1_w', 'o1_b', 'q2', 'k2', 'v2', 'o2_w', 'o2_b', 'ff_w1', 'ff_b1', 'ff_w2', 'ff_b2')}
    del _L1_xcond_all

    def _L2_xcond_setup():
        import jax, jax.numpy as jnp
        import numpy as np
        B, N, D, H, TD, TL = (4, 256, 256, 16, 192, 77)
        HD = D // H
        EPS = 1e-06

        def _ln(x):
            mu = jnp.mean(x, axis=-1, keepdims=True)
            var = jnp.var(x, axis=-1, keepdims=True)
            return (x - mu) * jax.lax.rsqrt(var + EPS)

        def _modulate(x, shift, scale):
            return x * (1.0 + scale[:, None, :]) + shift[:, None, :]

        def _heads(t):
            return t.reshape(t.shape[0], t.shape[1], H, HD).transpose(0, 2, 1, 3)

        def _attend(q, k, v):
            sim = jnp.einsum('bhid,bhjd->bhij', q, k) * HD ** (-0.5)
            attn = jax.nn.softmax(sim, axis=-1)
            out = jnp.einsum('bhij,bhjd->bhid', attn, v)
            return out.transpose(0, 2, 1, 3).reshape(out.shape[0], -1, D)
        key = jax.random.key(seed)
        ks = jax.random.split(key, 16)
        s = 0.02
        return {'x': jax.random.normal(ks[0], (B, N, D), jnp.float32), 'c': jax.random.normal(ks[1], (B, D), jnp.float32), 'text_embed': jax.random.normal(ks[2], (B, TL, TD), jnp.float32), 'W_ada': jax.random.normal(ks[3], (D, 6 * D), jnp.float32) * s, 'b_ada': jnp.zeros((6 * D,), jnp.float32), 'W_qkv': jax.random.normal(ks[4], (D, 3 * D), jnp.float32) * s, 'b_qkv': jnp.zeros((3 * D,), jnp.float32), 'W_proj': jax.random.normal(ks[5], (D, D), jnp.float32) * s, 'b_proj': jnp.zeros((D,), jnp.float32), 'W_ctx': jax.random.normal(ks[6], (TD, D), jnp.float32) * s, 'b_ctx': jnp.zeros((D,), jnp.float32), 'W_q': jax.random.normal(ks[7], (D, D), jnp.float32) * s, 'W_k': jax.random.normal(ks[8], (D, D), jnp.float32) * s, 'W_v': jax.random.normal(ks[9], (D, D), jnp.float32) * s, 'W_out': jax.random.normal(ks[10], (D, D), jnp.float32) * s, 'b_out': jnp.zeros((D,), jnp.float32), 'W_fc1': jax.random.normal(ks[11], (D, 4 * D), jnp.float32) * s, 'b_fc1': jnp.zeros((4 * D,), jnp.float32), 'W_fc2': jax.random.normal(ks[12], (4 * D, D), jnp.float32) * s, 'b_fc2': jnp.zeros((D,), jnp.float32)}
    _L2_xcond_all = _L2_xcond_setup()
    _L2_xcond_in = {k: v for k, v in _L2_xcond_all.items() if k in ('W_ada', 'b_ada', 'W_qkv', 'b_qkv', 'W_proj', 'b_proj', 'W_ctx', 'b_ctx', 'W_q', 'W_k', 'W_v', 'W_out', 'b_out', 'W_fc1', 'b_fc1', 'W_fc2', 'b_fc2')}
    del _L2_xcond_all

    def _L3_xcond_setup():
        import jax, jax.numpy as jnp
        import numpy as np
        D = 256
        CD = 192
        H = 16
        HD = D // H
        EPS = 1e-05

        def _ln(x, w, b):
            m = jnp.mean(x, axis=-1, keepdims=True)
            v = jnp.var(x, axis=-1, keepdims=True)
            return (x - m) * jax.lax.rsqrt(v + EPS) * w + b

        def _attn(q, k, v):
            q = q.reshape(q.shape[0], q.shape[1], H, HD).transpose(0, 2, 1, 3)
            k = k.reshape(k.shape[0], k.shape[1], H, HD).transpose(0, 2, 1, 3)
            v = v.reshape(v.shape[0], v.shape[1], H, HD).transpose(0, 2, 1, 3)
            scores = jnp.einsum('bhnd,bhmd->bhnm', q, k) * HD ** (-0.5)
            p = jax.nn.softmax(scores, axis=-1)
            o = jnp.einsum('bhnm,bhmd->bhnd', p, v)
            return o.transpose(0, 2, 1, 3).reshape(o.shape[0], o.shape[2], D)
        key = jax.random.key(seed)
        ks = iter(jax.random.split(key, 32))
        s = 0.02
        inp = {'x': jax.random.normal(next(ks), (4, 256, D), jnp.float32), 'context': jax.random.normal(next(ks), (4, 64, CD), jnp.float32), 'time_emb': jax.random.normal(next(ks), (4, D), jnp.float32), 'ln1_w': jnp.ones((D,)), 'ln1_b': jnp.zeros((D,)), 'ln2_w': jnp.ones((D,)), 'ln2_b': jnp.zeros((D,)), 'ln3_w': jnp.ones((D,)), 'ln3_b': jnp.zeros((D,)), 'Wqkv': jax.random.normal(next(ks), (D, 3 * D)) * s, 'bqkv': jnp.zeros((3 * D,)), 'Wos': jax.random.normal(next(ks), (D, D)) * s, 'bos': jnp.zeros((D,)), 'Wq': jax.random.normal(next(ks), (D, D)) * s, 'bq': jnp.zeros((D,)), 'Wk': jax.random.normal(next(ks), (CD, D)) * s, 'bk': jnp.zeros((D,)), 'Wv': jax.random.normal(next(ks), (CD, D)) * s, 'bv': jnp.zeros((D,)), 'Woc': jax.random.normal(next(ks), (D, D)) * s, 'boc': jnp.zeros((D,)), 'W1': jax.random.normal(next(ks), (D, 4 * D)) * s, 'b1': jnp.zeros((4 * D,)), 'W2': jax.random.normal(next(ks), (4 * D, D)) * s, 'b2': jnp.zeros((D,)), 'Wmod': jax.random.normal(next(ks), (D, 6 * D)) * s, 'bmod': jnp.zeros((6 * D,))}
        return inp
    _L3_xcond_all = _L3_xcond_setup()
    _L3_xcond_in = {k: v for k, v in _L3_xcond_all.items() if k in ('ln1_w', 'ln1_b', 'ln2_w', 'ln2_b', 'ln3_w', 'ln3_b', 'Wqkv', 'bqkv', 'Wos', 'bos', 'Wq', 'bq', 'Wk', 'bk', 'Wv', 'bv', 'Woc', 'boc', 'W1', 'b1', 'W2', 'b2', 'Wmod', 'bmod')}
    del _L3_xcond_all
    return {'x': x, 'cond_1024': cond_1024, 'ctx_768': ctx_768, 'L0_xcond_ln1_w': _L0_xcond_in['ln1_w'], 'L0_xcond_ln1_b': _L0_xcond_in['ln1_b'], 'L0_xcond_g1_w': _L0_xcond_in['g1_w'], 'L0_xcond_g1_b': _L0_xcond_in['g1_b'], 'L0_xcond_b1_w': _L0_xcond_in['b1_w'], 'L0_xcond_b1_b': _L0_xcond_in['b1_b'], 'L0_xcond_ln2_w': _L0_xcond_in['ln2_w'], 'L0_xcond_ln2_b': _L0_xcond_in['ln2_b'], 'L0_xcond_g2_w': _L0_xcond_in['g2_w'], 'L0_xcond_g2_b': _L0_xcond_in['g2_b'], 'L0_xcond_b2_w': _L0_xcond_in['b2_w'], 'L0_xcond_b2_b': _L0_xcond_in['b2_b'], 'L0_xcond_sa_wq': _L0_xcond_in['sa_wq'], 'L0_xcond_sa_wkv': _L0_xcond_in['sa_wkv'], 'L0_xcond_sa_wo': _L0_xcond_in['sa_wo'], 'L0_xcond_sa_bo': _L0_xcond_in['sa_bo'], 'L0_xcond_ca_lnc_w': _L0_xcond_in['ca_lnc_w'], 'L0_xcond_ca_lnc_b': _L0_xcond_in['ca_lnc_b'], 'L0_xcond_ca_wq': _L0_xcond_in['ca_wq'], 'L0_xcond_ca_wkv': _L0_xcond_in['ca_wkv'], 'L0_xcond_ca_wo': _L0_xcond_in['ca_wo'], 'L0_xcond_ca_bo': _L0_xcond_in['ca_bo'], 'L0_xcond_ff_w1': _L0_xcond_in['ff_w1'], 'L0_xcond_ff_b1': _L0_xcond_in['ff_b1'], 'L0_xcond_ff_w2': _L0_xcond_in['ff_w2'], 'L0_xcond_ff_b2': _L0_xcond_in['ff_b2'], 'L1_xcond_n1_w': _L1_xcond_in['n1_w'], 'L1_xcond_n1_b': _L1_xcond_in['n1_b'], 'L1_xcond_n2_w': _L1_xcond_in['n2_w'], 'L1_xcond_n2_b': _L1_xcond_in['n2_b'], 'L1_xcond_n3_w': _L1_xcond_in['n3_w'], 'L1_xcond_n3_b': _L1_xcond_in['n3_b'], 'L1_xcond_q1': _L1_xcond_in['q1'], 'L1_xcond_k1': _L1_xcond_in['k1'], 'L1_xcond_v1': _L1_xcond_in['v1'], 'L1_xcond_o1_w': _L1_xcond_in['o1_w'], 'L1_xcond_o1_b': _L1_xcond_in['o1_b'], 'L1_xcond_q2': _L1_xcond_in['q2'], 'L1_xcond_k2': _L1_xcond_in['k2'], 'L1_xcond_v2': _L1_xcond_in['v2'], 'L1_xcond_o2_w': _L1_xcond_in['o2_w'], 'L1_xcond_o2_b': _L1_xcond_in['o2_b'], 'L1_xcond_ff_w1': _L1_xcond_in['ff_w1'], 'L1_xcond_ff_b1': _L1_xcond_in['ff_b1'], 'L1_xcond_ff_w2': _L1_xcond_in['ff_w2'], 'L1_xcond_ff_b2': _L1_xcond_in['ff_b2'], 'L2_xcond_W_ada': _L2_xcond_in['W_ada'], 'L2_xcond_b_ada': _L2_xcond_in['b_ada'], 'L2_xcond_W_qkv': _L2_xcond_in['W_qkv'], 'L2_xcond_b_qkv': _L2_xcond_in['b_qkv'], 'L2_xcond_W_proj': _L2_xcond_in['W_proj'], 'L2_xcond_b_proj': _L2_xcond_in['b_proj'], 'L2_xcond_W_ctx': _L2_xcond_in['W_ctx'], 'L2_xcond_b_ctx': _L2_xcond_in['b_ctx'], 'L2_xcond_W_q': _L2_xcond_in['W_q'], 'L2_xcond_W_k': _L2_xcond_in['W_k'], 'L2_xcond_W_v': _L2_xcond_in['W_v'], 'L2_xcond_W_out': _L2_xcond_in['W_out'], 'L2_xcond_b_out': _L2_xcond_in['b_out'], 'L2_xcond_W_fc1': _L2_xcond_in['W_fc1'], 'L2_xcond_b_fc1': _L2_xcond_in['b_fc1'], 'L2_xcond_W_fc2': _L2_xcond_in['W_fc2'], 'L2_xcond_b_fc2': _L2_xcond_in['b_fc2'], 'L3_xcond_ln1_w': _L3_xcond_in['ln1_w'], 'L3_xcond_ln1_b': _L3_xcond_in['ln1_b'], 'L3_xcond_ln2_w': _L3_xcond_in['ln2_w'], 'L3_xcond_ln2_b': _L3_xcond_in['ln2_b'], 'L3_xcond_ln3_w': _L3_xcond_in['ln3_w'], 'L3_xcond_ln3_b': _L3_xcond_in['ln3_b'], 'L3_xcond_Wqkv': _L3_xcond_in['Wqkv'], 'L3_xcond_bqkv': _L3_xcond_in['bqkv'], 'L3_xcond_Wos': _L3_xcond_in['Wos'], 'L3_xcond_bos': _L3_xcond_in['bos'], 'L3_xcond_Wq': _L3_xcond_in['Wq'], 'L3_xcond_bq': _L3_xcond_in['bq'], 'L3_xcond_Wk': _L3_xcond_in['Wk'], 'L3_xcond_bk': _L3_xcond_in['bk'], 'L3_xcond_Wv': _L3_xcond_in['Wv'], 'L3_xcond_bv': _L3_xcond_in['bv'], 'L3_xcond_Woc': _L3_xcond_in['Woc'], 'L3_xcond_boc': _L3_xcond_in['boc'], 'L3_xcond_W1': _L3_xcond_in['W1'], 'L3_xcond_b1': _L3_xcond_in['b1'], 'L3_xcond_W2': _L3_xcond_in['W2'], 'L3_xcond_b2': _L3_xcond_in['b2'], 'L3_xcond_Wmod': _L3_xcond_in['Wmod'], 'L3_xcond_bmod': _L3_xcond_in['bmod']}

def reference(x, cond_1024, ctx_768, L0_xcond_ln1_w, L0_xcond_ln1_b, L0_xcond_g1_w, L0_xcond_g1_b, L0_xcond_b1_w, L0_xcond_b1_b, L0_xcond_ln2_w, L0_xcond_ln2_b, L0_xcond_g2_w, L0_xcond_g2_b, L0_xcond_b2_w, L0_xcond_b2_b, L0_xcond_sa_wq, L0_xcond_sa_wkv, L0_xcond_sa_wo, L0_xcond_sa_bo, L0_xcond_ca_lnc_w, L0_xcond_ca_lnc_b, L0_xcond_ca_wq, L0_xcond_ca_wkv, L0_xcond_ca_wo, L0_xcond_ca_bo, L0_xcond_ff_w1, L0_xcond_ff_b1, L0_xcond_ff_w2, L0_xcond_ff_b2, L1_xcond_n1_w, L1_xcond_n1_b, L1_xcond_n2_w, L1_xcond_n2_b, L1_xcond_n3_w, L1_xcond_n3_b, L1_xcond_q1, L1_xcond_k1, L1_xcond_v1, L1_xcond_o1_w, L1_xcond_o1_b, L1_xcond_q2, L1_xcond_k2, L1_xcond_v2, L1_xcond_o2_w, L1_xcond_o2_b, L1_xcond_ff_w1, L1_xcond_ff_b1, L1_xcond_ff_w2, L1_xcond_ff_b2, L2_xcond_W_ada, L2_xcond_b_ada, L2_xcond_W_qkv, L2_xcond_b_qkv, L2_xcond_W_proj, L2_xcond_b_proj, L2_xcond_W_ctx, L2_xcond_b_ctx, L2_xcond_W_q, L2_xcond_W_k, L2_xcond_W_v, L2_xcond_W_out, L2_xcond_b_out, L2_xcond_W_fc1, L2_xcond_b_fc1, L2_xcond_W_fc2, L2_xcond_b_fc2, L3_xcond_ln1_w, L3_xcond_ln1_b, L3_xcond_ln2_w, L3_xcond_ln2_b, L3_xcond_ln3_w, L3_xcond_ln3_b, L3_xcond_Wqkv, L3_xcond_bqkv, L3_xcond_Wos, L3_xcond_bos, L3_xcond_Wq, L3_xcond_bq, L3_xcond_Wk, L3_xcond_bk, L3_xcond_Wv, L3_xcond_bv, L3_xcond_Woc, L3_xcond_boc, L3_xcond_W1, L3_xcond_b1, L3_xcond_W2, L3_xcond_b2, L3_xcond_Wmod, L3_xcond_bmod):
    import jax
    import jax.numpy as jnp

    def _L0_xcond_ref(x, cond, context, ln1_w, ln1_b, g1_w, g1_b, b1_w, b1_b, ln2_w, ln2_b, g2_w, g2_b, b2_w, b2_b, sa_wq, sa_wkv, sa_wo, sa_bo, ca_lnc_w, ca_lnc_b, ca_wq, ca_wkv, ca_wo, ca_bo, ff_w1, ff_b1, ff_w2, ff_b2):
        import jax, jax.numpy as jnp
        import numpy as np
        B, N, M = (2, 256, 128)
        D, H, DH = (256, 16, 64)
        MID = H * DH
        DC = 192
        MULT = 4
        EPS = 1e-05

        def _ln(x, w, b):
            mu = jnp.mean(x, -1, keepdims=True)
            var = jnp.mean((x - mu) ** 2, -1, keepdims=True)
            return (x - mu) * jax.lax.rsqrt(var + EPS) * w + b

        def _sincos(n, d):
            inv = 1.0 / 10000.0 ** (jnp.arange(0, d, 2, dtype=jnp.float32) / d)
            ang = jnp.arange(n, dtype=jnp.float32)[:, None] * inv[None, :]
            return (jnp.sin(ang), jnp.cos(ang))

        def _rope(x, sin, cos):
            s = sin[None, None]
            c = cos[None, None]
            xe = x[..., ::2]
            xo = x[..., 1::2]
            re = xe * c - xo * s
            ro = xe * s + xo * c
            return jnp.stack((re, ro), axis=-1).reshape(x.shape)

        def _heads(t):
            b, n, _ = t.shape
            return t.reshape(b, n, H, DH).transpose(0, 2, 1, 3)

        def _attn(xq, ctx, wq, wkv, wo, bo):
            q = _heads(xq @ wq)
            k, v = jnp.split(ctx @ wkv, 2, axis=-1)
            k = _heads(k)
            v = _heads(v)
            sq, cq = _sincos(q.shape[2], DH)
            sk, ck = _sincos(k.shape[2], DH)
            q = _rope(q, sq, cq)
            k = _rope(k, sk, ck)
            sim = jnp.einsum('bhnd,bhmd->bhnm', q, k) * DH ** (-0.5)
            a = jax.nn.softmax(sim, axis=-1)
            o = jnp.einsum('bhnm,bhmd->bhnd', a, v)
            o = o.transpose(0, 2, 1, 3).reshape(xq.shape[0], xq.shape[1], MID)
            return o @ wo + bo

        def _adaln(x, c, lw, lb, gw, gb, bw, bb):
            g = (c @ gw + gb)[:, None, :]
            bt = (c @ bw + bb)[:, None, :]
            return _ln(x, lw, lb) * (1.0 + g) + bt
        attn_in = _adaln(x, cond, ln1_w, ln1_b, g1_w, g1_b, b1_w, b1_b)
        x = _attn(attn_in, attn_in, sa_wq, sa_wkv, sa_wo, sa_bo) + x
        cross_in = _adaln(x, cond, ln1_w, ln1_b, g1_w, g1_b, b1_w, b1_b)
        ctx_n = _ln(context, ca_lnc_w, ca_lnc_b)
        x = _attn(cross_in, ctx_n, ca_wq, ca_wkv, ca_wo, ca_bo) + x
        ffn_in = _adaln(x, cond, ln2_w, ln2_b, g2_w, g2_b, b2_w, b2_b)
        h = jax.nn.gelu(ffn_in @ ff_w1 + ff_b1, approximate=False)
        x = h @ ff_w2 + ff_b2 + x
        return x

    def _L1_xcond_ref(x, t, context, n1_w, n1_b, n2_w, n2_b, n3_w, n3_b, q1, k1, v1, o1_w, o1_b, q2, k2, v2, o2_w, o2_b, ff_w1, ff_b1, ff_w2, ff_b2):
        import jax, jax.numpy as jnp
        import numpy as np
        EPS = 1e-05

        def _ada_ln(x, t, W, b):
            emb = t @ W + b
            scale, shift = jnp.split(emb, 2, axis=-1)
            mu = x.mean(-1, keepdims=True)
            var = ((x - mu) ** 2).mean(-1, keepdims=True)
            xn = (x - mu) * jax.lax.rsqrt(var + EPS)
            return xn * (1.0 + scale) + shift

        def _attn(x, ctx, Wq, Wk, Wv, Wo, bo, heads):
            b, n, _ = x.shape
            j = ctx.shape[1]
            q = (x @ Wq).reshape(b, n, heads, -1)
            k = (ctx @ Wk).reshape(b, j, heads, -1)
            v = (ctx @ Wv).reshape(b, j, heads, -1)
            scale = q.shape[-1] ** (-0.5)
            sim = jnp.einsum('bihd,bjhd->bhij', q, k) * scale
            attn = jax.nn.softmax(sim, axis=-1)
            out = jnp.einsum('bhij,bjhd->bihd', attn, v).reshape(b, n, -1)
            return out @ Wo + bo

        def _ff(x, W1, b1, W2, b2):
            p = x @ W1 + b1
            a, gate = jnp.split(p, 2, axis=-1)
            return a * jax.nn.gelu(gate, approximate=False) @ W2 + b2
        H = 16
        h = _ada_ln(x, t, n1_w, n1_b)
        x = _attn(h, h, q1, k1, v1, o1_w, o1_b, H) + x
        h = _ada_ln(x, t, n2_w, n2_b)
        x = _attn(h, context, q2, k2, v2, o2_w, o2_b, H) + x
        h = _ada_ln(x, t, n3_w, n3_b)
        x = _ff(h, ff_w1, ff_b1, ff_w2, ff_b2) + x
        return x

    def _L2_xcond_ref(x, c, text_embed, W_ada, b_ada, W_qkv, b_qkv, W_proj, b_proj, W_ctx, b_ctx, W_q, W_k, W_v, W_out, b_out, W_fc1, b_fc1, W_fc2, b_fc2):
        import jax, jax.numpy as jnp
        import numpy as np
        B, N, D, H, TD, TL = (4, 256, 256, 16, 192, 77)
        HD = D // H
        EPS = 1e-06

        def _ln(x):
            mu = jnp.mean(x, axis=-1, keepdims=True)
            var = jnp.var(x, axis=-1, keepdims=True)
            return (x - mu) * jax.lax.rsqrt(var + EPS)

        def _modulate(x, shift, scale):
            return x * (1.0 + scale[:, None, :]) + shift[:, None, :]

        def _heads(t):
            return t.reshape(t.shape[0], t.shape[1], H, HD).transpose(0, 2, 1, 3)

        def _attend(q, k, v):
            sim = jnp.einsum('bhid,bhjd->bhij', q, k) * HD ** (-0.5)
            attn = jax.nn.softmax(sim, axis=-1)
            out = jnp.einsum('bhij,bhjd->bhid', attn, v)
            return out.transpose(0, 2, 1, 3).reshape(out.shape[0], -1, D)
        mod = jax.nn.silu(c) @ W_ada + b_ada
        sh_msa, sc_msa, sh_x, sc_x, sh_mlp, sc_mlp = jnp.split(mod, 6, axis=-1)
        h1 = _modulate(_ln(x), sh_msa, sc_msa)
        qkv = h1 @ W_qkv + b_qkv
        q, k, v = jnp.split(qkv, 3, axis=-1)
        out = _attend(_heads(q), _heads(k), _heads(v))
        x = x + (out @ W_proj + b_proj)
        h2 = _modulate(_ln(x), sh_x, sc_x)
        ctx = text_embed @ W_ctx + b_ctx
        q = _heads(h2 @ W_q)
        k = _heads(ctx @ W_k)
        v = _heads(ctx @ W_v)
        out = _attend(q, k, v)
        x = x + (out @ W_out + b_out)
        h3 = _modulate(_ln(x), sh_mlp, sc_mlp)
        hidden = jax.nn.gelu(h3 @ W_fc1 + b_fc1, approximate=True)
        x = x + (hidden @ W_fc2 + b_fc2)
        return x

    def _L3_xcond_ref(x, context, time_emb, ln1_w, ln1_b, ln2_w, ln2_b, ln3_w, ln3_b, Wqkv, bqkv, Wos, bos, Wq, bq, Wk, bk, Wv, bv, Woc, boc, W1, b1, W2, b2, Wmod, bmod):
        import jax, jax.numpy as jnp
        import numpy as np
        D = 256
        CD = 192
        H = 16
        HD = D // H
        EPS = 1e-05

        def _ln(x, w, b):
            m = jnp.mean(x, axis=-1, keepdims=True)
            v = jnp.var(x, axis=-1, keepdims=True)
            return (x - m) * jax.lax.rsqrt(v + EPS) * w + b

        def _attn(q, k, v):
            q = q.reshape(q.shape[0], q.shape[1], H, HD).transpose(0, 2, 1, 3)
            k = k.reshape(k.shape[0], k.shape[1], H, HD).transpose(0, 2, 1, 3)
            v = v.reshape(v.shape[0], v.shape[1], H, HD).transpose(0, 2, 1, 3)
            scores = jnp.einsum('bhnd,bhmd->bhnm', q, k) * HD ** (-0.5)
            p = jax.nn.softmax(scores, axis=-1)
            o = jnp.einsum('bhnm,bhmd->bhnd', p, v)
            return o.transpose(0, 2, 1, 3).reshape(o.shape[0], o.shape[2], D)
        mod = jax.nn.silu(time_emb) @ Wmod + bmod
        sh1, sc1, sh2, sc2, sh3, sc3 = jnp.split(mod, 6, axis=-1)
        h = _ln(x, ln1_w, ln1_b) * (1 + sc1[:, None, :]) + sh1[:, None, :]
        qkv = h @ Wqkv + bqkv
        q, k, v = jnp.split(qkv, 3, axis=-1)
        x = x + _attn(q, k, v) @ Wos + bos
        h = _ln(x, ln2_w, ln2_b) * (1 + sc2[:, None, :]) + sh2[:, None, :]
        x = x + _attn(h @ Wq + bq, context @ Wk + bk, context @ Wv + bv) @ Woc + boc
        h = _ln(x, ln3_w, ln3_b) * (1 + sc3[:, None, :]) + sh3[:, None, :]
        x = x + jax.nn.gelu(h @ W1 + b1, approximate=False) @ W2 + b2
        return x
    x = _L0_xcond_ref(x, cond_1024, ctx_768, L0_xcond_ln1_w, L0_xcond_ln1_b, L0_xcond_g1_w, L0_xcond_g1_b, L0_xcond_b1_w, L0_xcond_b1_b, L0_xcond_ln2_w, L0_xcond_ln2_b, L0_xcond_g2_w, L0_xcond_g2_b, L0_xcond_b2_w, L0_xcond_b2_b, L0_xcond_sa_wq, L0_xcond_sa_wkv, L0_xcond_sa_wo, L0_xcond_sa_bo, L0_xcond_ca_lnc_w, L0_xcond_ca_lnc_b, L0_xcond_ca_wq, L0_xcond_ca_wkv, L0_xcond_ca_wo, L0_xcond_ca_bo, L0_xcond_ff_w1, L0_xcond_ff_b1, L0_xcond_ff_w2, L0_xcond_ff_b2)
    x = _L1_xcond_ref(x, cond_1024[:, None, :], ctx_768, L1_xcond_n1_w, L1_xcond_n1_b, L1_xcond_n2_w, L1_xcond_n2_b, L1_xcond_n3_w, L1_xcond_n3_b, L1_xcond_q1, L1_xcond_k1, L1_xcond_v1, L1_xcond_o1_w, L1_xcond_o1_b, L1_xcond_q2, L1_xcond_k2, L1_xcond_v2, L1_xcond_o2_w, L1_xcond_o2_b, L1_xcond_ff_w1, L1_xcond_ff_b1, L1_xcond_ff_w2, L1_xcond_ff_b2)
    x = _L2_xcond_ref(x, cond_1024, ctx_768, L2_xcond_W_ada, L2_xcond_b_ada, L2_xcond_W_qkv, L2_xcond_b_qkv, L2_xcond_W_proj, L2_xcond_b_proj, L2_xcond_W_ctx, L2_xcond_b_ctx, L2_xcond_W_q, L2_xcond_W_k, L2_xcond_W_v, L2_xcond_W_out, L2_xcond_b_out, L2_xcond_W_fc1, L2_xcond_b_fc1, L2_xcond_W_fc2, L2_xcond_b_fc2)
    x = _L3_xcond_ref(x, ctx_768, cond_1024, L3_xcond_ln1_w, L3_xcond_ln1_b, L3_xcond_ln2_w, L3_xcond_ln2_b, L3_xcond_ln3_w, L3_xcond_ln3_b, L3_xcond_Wqkv, L3_xcond_bqkv, L3_xcond_Wos, L3_xcond_bos, L3_xcond_Wq, L3_xcond_bq, L3_xcond_Wk, L3_xcond_bk, L3_xcond_Wv, L3_xcond_bv, L3_xcond_Woc, L3_xcond_boc, L3_xcond_W1, L3_xcond_b1, L3_xcond_W2, L3_xcond_b2, L3_xcond_Wmod, L3_xcond_bmod)
    return x

_drawn_inputs = setup_inputs


def setup_inputs(seed=0):
    import zlib

    import numpy as np

    out = dict(_drawn_inputs(seed))
    spreads = {'L0_xcond_ln1_w': (1.0, 0.6),
     'L0_xcond_ln1_b': (0.0, 0.389),
     'L0_xcond_g1_b': (0.0, 0.8),
     'L0_xcond_b1_b': (0.0, 0.36),
     'L0_xcond_ln2_w': (1.0, 0.6),
     'L0_xcond_ln2_b': (0.0, 0.665),
     'L0_xcond_g2_b': (0.0, 0.729),
     'L0_xcond_b2_b': (0.0, 0.788),
     'L0_xcond_sa_bo': (0.0, 0.1),
     'L0_xcond_ca_lnc_w': (1.0, 0.6),
     'L0_xcond_ca_lnc_b': (0.0, 0.53),
     'L0_xcond_ca_bo': (0.0, 0.1),
     'L0_xcond_ff_b1': (0.0, 0.1),
     'L0_xcond_ff_b2': (0.0, 0.1),
     'L1_xcond_n1_b': (0.0, 0.413),
     'L1_xcond_n2_b': (0.0, 0.8),
     'L1_xcond_n3_b': (0.0, 0.8),
     'L1_xcond_o1_b': (0.0, 0.1),
     'L1_xcond_o2_b': (0.0, 0.1),
     'L1_xcond_ff_b1': (0.0, 0.472),
     'L1_xcond_ff_b2': (0.0, 0.1),
     'L2_xcond_b_ada': (0.0, 0.476),
     'L2_xcond_b_qkv': (0.0, 0.267),
     'L2_xcond_b_proj': (0.0, 0.1),
     'L2_xcond_b_ctx': (0.0, 0.8),
     'L2_xcond_b_out': (0.0, 0.1),
     'L2_xcond_b_fc1': (0.0, 0.507),
     'L2_xcond_b_fc2': (0.0, 0.1),
     'L3_xcond_ln1_w': (1.0, 0.6),
     'L3_xcond_ln1_b': (0.0, 0.799),
     'L3_xcond_ln2_w': (1.0, 0.6),
     'L3_xcond_ln2_b': (0.0, 0.8),
     'L3_xcond_ln3_w': (1.0, 0.6),
     'L3_xcond_ln3_b': (0.0, 0.724),
     'L3_xcond_bqkv': (0.0, 0.271),
     'L3_xcond_bos': (0.0, 0.1),
     'L3_xcond_bq': (0.0, 2.0),
     'L3_xcond_bk': (0.0, 2.0),
     'L3_xcond_bv': (0.0, 0.267),
     'L3_xcond_boc': (0.0, 0.1),
     'L3_xcond_b1': (0.0, 0.46),
     'L3_xcond_b2': (0.0, 0.1),
     'L3_xcond_bmod': (0.0, 0.453)}
    factors = {'L0_xcond_g1_w': 7.469,
     'L0_xcond_sa_wq': 8.0,
     'L0_xcond_ca_wq': 8.0,
     'L1_xcond_n2_w': 8.0,
     'L1_xcond_q1': 8.0,
     'L1_xcond_k1': 8.0,
     'L1_xcond_q2': 8.0,
     'L1_xcond_k2': 8.0,
     'L2_xcond_W_ctx': 4.216,
     'L2_xcond_W_q': 8.0,
     'L2_xcond_W_k': 8.0,
     'L2_xcond_W_v': 3.393,
     'L2_xcond_W_out': 3.596,
     'L3_xcond_Wq': 8.0,
     'L3_xcond_Wk': 8.0}
    for name, (base, spread) in spreads.items():
        noise = np.random.default_rng([zlib.crc32(name.encode()), seed]).standard_normal(out[name].shape)
        drawn = base * np.exp(spread * noise) if base else spread * noise
        out[name] = jnp.asarray(drawn.astype(out[name].dtype))
    for name, factor in factors.items():
        out[name] = (out[name] * factor).astype(out[name].dtype)
    return out
```

```python
from contextlib import ExitStack

import concourse.bass as bass
from concourse import mybir

F32 = mybir.dt.float32
F16 = mybir.dt.float16
ALU = mybir.AluOpType
ACT = mybir.ActivationFunctionType
AXX = mybir.AxisListType.X

P = 128
B = 8
N = 256
D = 256
DT = D // P
TT = N // P
H = 16
M = 77
DC = 192
CP = DC // 2
FF = 4 * D
FT = FF // P
START = -1
RING = 2
HI, LO = 0, 1


class Stage:
    pass


def plan_stages():
    stages = []
    products = 2 * 4 + B
    units = tiles = rotated = pairs = key_heads = activations = splits = chunks = 0
    for layer in range(4):
        dh = 64 if layer < 2 else 16
        for kind in ("self", "cross", "ff"):
            st = Stage()
            st.index, st.layer, st.kind = len(stages), layer, kind
            st.dh, st.nt = dh, H * dh // P
            st.hpt = H // st.nt
            st.rope = layer == 0 and kind != "ff"
            st.product0, st.unit0, st.tile0, st.rotated0 = products, units, tiles, rotated
            st.norm0 = (B + 1) * st.index
            if kind == "ff":
                if layer == 1:
                    order = [(w, f) for f in range(FT) for w in ("gate", "up")]
                else:
                    order = [("gelu", f) for f in range(FT)]
                st.units = 0
            else:
                order = [("ctx", t) for t in range(2)] if (layer, kind) == (2, "cross") else []
                if st.rope:
                    items = [("raw", i) for i in range(2 * st.nt)]
                    order += items[:2]
                    for i in range(2 * st.nt):
                        order += [("rot", i)] + items[i + 2:i + 3]
                elif kind == "cross" and st.nt == 8:
                    order += [("q", 0), ("k", 0), ("q", 1), ("q", 2), ("k", 1), ("q", 3)]
                else:
                    order += [(w, t) for t in range(st.nt // 2) for w in ("q", "k")]
                st.key_tiles = 4 if kind == "cross" and st.nt == 8 else 2
                st.value_cuts = 1 if st.nt == 2 and kind == "self" else 2
                st.values = (TT if kind == "self" else 1) * st.value_cuts
                order += [("v", c) for c in range(st.values)]
                st.units = H if kind == "self" else H // 2
                units += B * st.units
                tiles += B * st.nt
                if st.rope:
                    rotated += B * st.nt
            turned = [("h", d) for d in range(DT)]
            if kind == "ff":
                at = len(order) * 3 // 4
                order = order[:at] + turned[:1] + order[at:at + 1] + turned[1:] + order[at + 1:]
            else:
                order += turned
            order += [("out", t) for t in range(TT)]
            assert len(order) % 2 == 0
            st.order = order
            st.place = {p: i for i, p in enumerate(order)}
            st.paired = [p for p in order if p[0] in ("ctx", "q", "k", "v")]
            st.pair0, st.key0, st.act0 = pairs, key_heads, activations
            pairs += B * len(st.paired)
            if kind == "ff":
                activations += B * FT
            else:
                key_heads += B * H
            products += DT + B * len(order)
            st.columns = {"self": 3 * DT * st.nt * P + st.nt * D, "cross": 3 * DT * st.nt * P + st.nt * D,
                          "ff": (2 if layer == 1 else 1) * DT * FF + FT * D}[kind]
            if (layer, kind) == (2, "cross"):
                st.columns += 2 * D
            stages.append(st)
    for st in stages:
        ahead = {"self": [2], "cross": [2], "ff": [2]}[st.kind]
        if st.index == 0:
            ahead = [1, 2]
        st.jobs = [stages[st.index + a] for a in ahead if st.index + a < len(stages)]
        st.split0, st.chunk0 = splits, chunks
        splits += B if st.jobs else 0
        chunks += B * len(st.jobs)
    return stages


def high(st, b, what):
    return b * len(st.paired) + (st.pair0 + st.paired.index(what) + 1)


def made(st, b, what):
    if b is START:
        return st.product0 + what[1] + 1
    return b * len(st.order) + (st.product0 + DT + st.place[what] + 1)


def used(st, b, what):
    if b is START:
        return (st.product0 + what[1]) // 2
    return b * (len(st.order) // 2) + (st.product0 + DT + st.place[what]) // 2


def wait_stream(engine, product_taken, st, b):
    for tok in range(TT):
        engine.wait_ge(product_taken[bank_of(st, ("out", tok))], used(st, b, ("out", tok)) + 1)


def bank_of(st, what):
    return st.place[what] % 2


def build(nc, A, out):
    STAGES = plan_stages()
    with ExitStack() as ctx:
        def sb(name, shape):
            return ctx.enter_context(nc.sbuf_tensor(name, shape, F32))

        def psum(name, shape):
            return ctx.enter_context(nc.psum_tensor(name, shape, F32))

        def sem(name):
            return ctx.enter_context(nc.semaphore(name))

        x = sb("x", [P, B + 1, TT, D])
        weights_at = {"self": sb("self_w", [P, 8192]), "cross": sb("cross_w", [P, 8192]), "ff": sb("ff_w", [P, 6144])}
        staging = sb("staging", [P, 1536])

        def pair(region, *dims):
            names = [f"d{i}" for i in range(len(dims))]
            v = region[:].bitcast(F16) if len(region.shape) == 2 else None
            return v.rearrange(f"p (part {' '.join(names)}) -> p part {' '.join(names)}", part=2,
                               **dict(zip(names, dims)))

        keys_r, values_r = sb("keys", [P, H * N]), sb("values", [P, TT * H * P])
        tall_r = sb("tall", [P, 8 * N])
        keys = keys_r[:].bitcast(F16).rearrange("p (h part n) -> p h part n", h=H, part=2)
        values = pair(values_r, TT, H, P)
        queries_r = sb("queries", [P, 8 * N])
        queries = pair(queries_r, 8, N)
        tall = pair(tall_r, 8, N)
        hidden = pair(sb("hidden", [P, DT * N]), DT, N)
        hidden32 = sb("hidden32", [P, DT, N])
        probs = sb("probs", [P, 4, 512])
        probs_t = sb("probs_t", [P, 2 * 512])[:].bitcast(F16).rearrange("p (r part n) -> p r part n", r=2, part=2)
        key_tile = sb("key_tile", [P, 4 * N])[:].bitcast(F16).rearrange("p (r part n) -> p r part n", r=4, part=2)
        xn = sb("xn", [P, TT, D])
        ident = sb("ident", [P, P])
        cos_t = sb("cos_t", [P, N])
        sin_t = sb("sin_t", [P, N])
        rot_m = sb("rot_m", [P, P])
        raw = sb("raw", [P, 2, N])
        gated = raw
        work = sb("work", [P, 4, N])
        by_cos, by_sin = work[:, 0:2], work[:, 2:4]
        sum32 = hidden32
        ctx_all = sb("ctx_all", [CP, B + 1, 2, M])
        ctx_b = sb("ctx_b", [CP, 2 * M])[:].bitcast(F16).rearrange("p (part k m) -> p part k m", part=2, k=2)
        ctx_p = sb("ctx_p", [P, DT * M])[:].bitcast(F16).rearrange("p (part k m) -> p part k m", part=2, k=2)
        ctx_tok = probs[0:M, 0:3, :].rearrange("p a n -> p (a n)").rearrange("p (b d) -> p b d", b=B)
        NV = A["vectors"].shape[1]
        vec = sb("vec", [P, NV])
        NR = A["rows0"].shape[1]
        rows = sb("rows", [P, 2, NR])
        cond = sb("cond", [P, 2, DT, B])
        mod_sb = queries_r[:, 0:384].rearrange("p (l g b) -> p l g b", l=4, g=12)
        mod_tmp = queries_r[:, 384:576].rearrange("p (l n d b) -> p l n d b", l=4, n=3, d=DT)
        cbn = queries_r[0:M, 704:752].rearrange("p (b s) -> p b s", b=B)
        cmv = queries_r[0:M, 752:768].rearrange("p (b s) -> p b s", b=B)
        crs = queries_r[0:M, 768:784].rearrange("p (a b) -> p a b", a=2)
        gain = sb("gain", [P, 4, 3, DT, B + 1])
        shift = sb("shift", [P, 4, 3, DT, B + 1])
        mod_w = [tall_r[:, 0:2048], weights_at["ff"][:, 0:3072], weights_at["ff"][:, 3072:6144],
                 weights_at["cross"][:, 0:3072]]
        mod_w = [m.rearrange("p (k n) -> p k n", k=DT) for m in mod_w]
        first_w = [keys_r[:, 0:2048], keys_r[:, 2048:4096], values_r[:, 0:2048], values_r[:, 2048:4096]]
        bn = sb("bn", [P, TT, 6])
        wait_carrier = sb("wait_carrier", [P, 1])
        pool_carrier = sb("pool_carrier", [P, 3])
        table_warm = sb("table_warm", [P, 1])
        mv = sb("mv", [P, TT, 2])
        var_eps = sb("var_eps", [P, TT])
        rstd = sb("rstd", [P, TT])
        minus_half = sb("minus_half", [P, 8])
        epsilons = sb("epsilons", [P, 2, TT])
        neg_max = sb("neg_max", [P, 4, 4])
        sums = sb("sums", [P, 4, 4])
        recips = sb("recips", [P, 4, 4])

        scores = [psum(f"scores{i}", [P, 512]) for i in range(2)]
        turned = [psum(f"turned{i}", [P, 512]) for i in range(2)]
        heads_out = [psum(f"heads_out{i}", [P, 512]) for i in range(2)]
        prod = [psum(f"prod{i}", [P, 512]) for i in range(2)]

        consts_in = sem("consts_in")
        x_in = sem("x_in")
        mod_w_in = [sem(f"mod_w_in{i}") for i in range(4)]
        first_w_in = [sem(f"first_w_in{i}") for i in range(4)]
        first_high = sem("first_high")
        first_split = sem("first_split")
        chunk_in = sem("chunk_in")
        chunk_high = sem("chunk_high")
        chunk_split = sem("chunk_split")
        rows_in = [sem("rows_in_even"), sem("rows_in_odd")]
        ctx_in = sem("ctx_in")
        out_written = sem("out_written")
        buffers_set = sem("buffers_set")
        values_zeroed = sem("values_zeroed")
        silu_step = sem("silu_step")
        product_made = sem("product_made")
        product_taken = [sem("product_taken0"), sem("product_taken1")]
        mod_step = sem("mod_step")
        mod_made = sem("mod_made")
        cn_step = sem("cn_step")
        cn_rstd = sem("cn_rstd")
        cn_made = sem("cn_made")
        bn_made = sem("bn_made")
        stats_made = sem("stats_made")
        eps_added = sem("eps_added")
        rstd_made = sem("rstd_made")
        xn_made = sem("xn_made")
        bias_added = sem("bias_added")
        ctx_copied = sem("ctx_copied")
        high_made = sem("high_made")
        cos_made = sem("cos_made")
        summed = sem("summed")
        sum_high = sem("sum_high")
        sum_split = sem("sum_split")
        keys_made = sem("keys_made")
        hidden_high = sem("hidden_high")
        hidden_made = sem("hidden_made")
        act_high = sem("act_high")
        act_made = sem("act_made")
        turned_high = sem("turned_high")
        heads_high = sem("heads_high")
        ctx_high = sem("ctx_high")
        scores_made = sem("scores_made")
        max_made = sem("max_made")
        exp_made = sem("exp_made")
        recip_made = sem("recip_made")
        probs_made = sem("probs_made")
        turned_made = sem("turned_made")
        turned_taken = sem("turned_taken")
        heads_made = sem("heads_made")
        heads_taken = sem("heads_taken")

        V = A["_vec_at"]

        def col(name, i=0):
            return vec[:, V[name] + i:V[name] + i + 1]

        def row(st, name):
            i = A["_row_at"][name]
            return rows[:, st.layer % 2, i * D:(i + 1) * D]

        def mask(st, j):
            c = V["mask2" if st.hpt == 2 else "mask8"] + j
            return vec[:, c:c + 1]

        def bias_of(st, what):
            name = f"{st.kind}_{what}b{st.layer}"
            return name if name in V else None

        def split_weights(st):
            w = weights_at[st.kind][:].bitcast(F16)
            half = weights_at[st.kind].shape[1]
            return [w[:, 0:half], w[:, half:2 * half]]

        def weights(st):
            n, found = st.nt * P, []
            for w in split_weights(st):
                cuts = [w[:, i * DT * n:(i + 1) * DT * n].rearrange("p (k n) -> p k n", k=DT) for i in range(3)]
                at = 3 * DT * n
                o = w[:, at:at + st.nt * D].rearrange("p (t n) -> p t n", t=st.nt)
                c = w[0:CP, at + st.nt * D:at + st.nt * D + 2 * D].rearrange("p (k n) -> p k n", k=2) \
                    if (st.layer, st.kind) == (2, "cross") else None
                found.append((*cuts, o, c))
            return found

        def ff_weights(st):
            f = FF * (2 if st.layer == 1 else 1)
            return [(w[:, 0:DT * f].rearrange("p (k n) -> p k n", k=DT),
                     w[:, DT * f:DT * f + FT * D].rearrange("p (t n) -> p t n", t=FT)) for w in split_weights(st)]

        def value_slots(st, part, kt, half, rows_n):
            v = values[0:rows_n, part, kt]
            if st.value_cuts == 1 or st.hpt == 2:
                dims = [[st.hpt * P, H // st.value_cuts // st.hpt], [P + st.dh, st.hpt], [1, st.dh]]
            else:
                dims = [[P + st.dh, 8], [1, st.dh]]
            return bass.AP(tensor=v.tensor, offset=v.offset + half * 8 * P, ap=[list(v.ap[0])] + dims)

        def value_source(st, ap):
            if st.value_cuts == 1 or st.hpt == 2:
                return ap.rearrange("p (t j e) -> p t j e", j=st.hpt, e=st.dh)
            return ap.rearrange("p (j e) -> p j e", e=st.dh)

        def row_width(st):
            return N if st.kind == "self" else M

        def n_rows(st):
            return TT if st.kind == "self" else 2 * TT

        def summed_when(st, b, i):
            return b * (2 * st.nt) + (2 * st.rotated0 + RING + i + 1)

        def keys_when(st, b, h):
            return b * H + (st.key0 + H + h + 1)

        def tile_keys_when(st, b, t):
            return keys_when(st, b, (t + 1) * st.hpt - 1)

        def values_at(st, step):
            if st.nt == 2:
                return range(st.values) if step == 0 else ()
            return range(st.values // 2) if step == 1 else range(st.values // 2, st.values) if step == 2 else ()

        def cos_when(st, b, i):
            return b * (2 * st.nt) + (2 * st.rotated0 + RING + i + 1)

        def unit_tile(st, u):
            return (u if st.kind == "self" else 2 * u) // st.hpt

        def ends_tile(st, u):
            return u == st.units - 1 or unit_tile(st, u + 1) != unit_tile(st, u)

        def starts_tile(st, u):
            return u == 0 or unit_tile(st, u - 1) != unit_tile(st, u)

        def next_at(st):
            return 4 if st.kind == "self" else 1
        block = ctx.enter_context(nc.Block())

        @block.sync
        def _(sp):
            for name, dst in (("ident", ident), ("vectors", vec)):
                sp.dma_start(dst[:], A[name]).then_inc(consts_in, 16)
            sp.dma_start(cond[:, 0], A["cond_t"]).then_inc(consts_in, 16)
            sp.dma_start(mod_w[0], A["mod_w0"].rearrange("(k p) n -> p k n", p=P)).then_inc(mod_w_in[0], 16)
            sp.dma_start(ctx_tok, A["ctx"]).then_inc(ctx_in, 16)
            for i in range(4):
                sp.dma_start(first_w[i], A["w0"][:, 2048 * i:2048 * (i + 1)]).then_inc(first_w_in[i], 16)
            sp.dma_start(x[:, 0:B], A["x"].rearrange("b (t p) d -> p b t d", p=P)).then_inc(x_in, 16)
            for name, dst in (("rot_m", rot_m[:]), ("cos_t", cos_t[:]), ("sin_t", sin_t[:])):
                sp.dma_start(dst, A[name]).then_inc(consts_in, 16)
            for layer in range(1, 4):
                sp.dma_start(mod_w[layer], A[f"mod_w{layer}"].rearrange("(k p) n -> p k n", p=P)).then_inc(mod_w_in[layer], 16)
            for st in STAGES:
                layer = st.layer
                if st.kind == "self":
                    if layer >= 2:
                        sp.wait_ge(bias_added, STAGES[3 * layer - 3].norm0)
                    sp.dma_start(rows[:, layer % 2, :], A[f"rows{layer}"][0].partition_broadcast(P)).then_inc(rows_in[layer % 2], 16)
                if (layer, st.kind) == (0, "ff"):
                    wait_stream(sp, product_taken, STAGES[1], B - 1)
                    sp.dma_start(ctx_all[:, 0:B], A["ctx_t"]).then_inc(ctx_in, 16)
                if st.jobs:
                    with sp.Fori(0, B) as b:
                        sp.wait_ge(chunk_split, b + (st.split0 + 1))
                        at = 0
                        for job in st.jobs:
                            c = job.columns // B
                            sp.dma_start(staging[:, at:at + c], A[f"w{job.index}"][:, bass.ds(b * c, c)]).then_inc(chunk_in, 16)
                            at += c
            last = STAGES[-1]
            to = out.rearrange("b (t p) d -> p b t d", p=P)
            with sp.Fori(0, B) as b:
                wait_stream(sp, product_taken, last, b)
                sp.dma_start(to[:, bass.ds(b, 1)], x[:, bass.ds(b, 1)]).then_inc(out_written, 16)
            sp.wait_ge(out_written, 16 * B)

        @block.tensor
        def _(pe):
            def turn_hidden(st, b, width_tiles):
                pe.wait_ge(xn_made, b + (st.norm0 + 2))
                for d in width_tiles:
                    bank = bank_of(st, ("h", d)) if b is not START else d % 2
                    pe.wait_ge(product_taken[bank], used(st, b, ("h", d)))
                    for t in range(TT):
                        last = nc.tensor.transpose(prod[bank][:, t * P:(t + 1) * P],
                                                   xn[:, t, d * P:(d + 1) * P], ident[:])
                    last.then_inc(product_made, 1)

            def wait_taken(st, b, what):
                if b is START:
                    pe.wait_ge(product_taken[what[1] % 2], used(st, b, what) + 1)
                else:
                    pe.wait_ge(product_taken[bank_of(st, what)], used(st, b, what) + 1)

            def product(o, left, right, start, stop):
                nc.tensor.matmul(o, left[HI], right[HI], start=start, stop=False)
                nc.tensor.matmul(o, left[HI], right[LO], start=False, stop=False)
                return nc.tensor.matmul(o, left[LO], right[HI], start=False, stop=stop)

            def modulation(layer, at):
                pe.wait_ge(mod_w_in[layer], 16)
                if layer == 2:
                    pe.wait_ge(silu_step, 4)
                nm = A[f"mod_w{layer}"].shape[1] // D
                c = cond[:, 0 if layer < 2 else 1]
                for half in range(2):
                    if at:
                        pe.wait_ge(product_taken[half], at // 2)
                    for j in range(nm):
                        g = half * nm + j
                        for k in range(DT):
                            last = nc.tensor.matmul(prod[half][:, j * B:(j + 1) * B],
                                                    mod_w[layer][:, k, g * P:(g + 1) * P], c[:, k],
                                                    start=(k == 0), stop=(k == DT - 1))
                    last.then_inc(product_made, 1)

            def projections(st, b, whats):
                w = weights(st)
                wq, wk, wv, wo, wc = [[part[i] for part in w] for i in range(5)]
                source = hidden if st.kind == "self" else ctx_p if st.layer == 2 else ctx_b
                rows_k = P if st.kind == "self" or st.layer == 2 else CP
                width = row_width(st)
                for what in whats:
                    name, i = what
                    bank = bank_of(st, what)
                    g = prod[bank]
                    if name == "k" and i == 0 and st.layer == 2 and st.kind == "cross":
                        wait_taken(st, b, ("ctx", 0))
                        wait_taken(st, b, ("ctx", 1))
                    if name == "rot":
                        wait_taken(st, b, ("raw", i))
                    pe.wait_ge(product_taken[bank], used(st, b, what))
                    if name == "rot":
                        n = N if i < st.nt else width
                        nc.tensor.matmul(g[:, 0:n], rot_m[:], raw[:, i % 2, 0:n],
                                         start=True, stop=True).then_inc(product_made, 1)
                        continue
                    is_q = name == "q" or (name == "raw" and i < st.nt)
                    if name == "v":
                        wide = st.nt * P // st.value_cuts
                        kt, cut = i // st.value_cuts, i % st.value_cuts
                        n_keys = min(P, width)
                        for k in range(2):
                            last = product(g[0:n_keys, 0:wide],
                                           [source[:, p, k, kt * P:kt * P + n_keys] for p in range(2)],
                                           [wv[p][0:rows_k, k, cut * wide:(cut + 1) * wide] for p in range(2)],
                                           k == 0, k == 1)
                        last.then_inc(product_made, 1)
                        continue
                    n = M if name == "ctx" else N if is_q else width
                    if name in ("q", "k"):
                        many = 2 if name == "q" else st.key_tiles
                        tiles = range(many * i, many * (i + 1))
                    else:
                        tiles = [i % st.nt]
                    for j, t in enumerate(tiles):
                        cols = slice(t * P, (t + 1) * P)
                        for k in range(2):
                            if name == "ctx":
                                left, right = [wc[p][:, k, cols] for p in range(2)], [ctx_b[:, p, k] for p in range(2)]
                            elif is_q:
                                left, right = [wq[p][:, k, cols] for p in range(2)], [hidden[:, p, k] for p in range(2)]
                            else:
                                left = [wk[p][0:rows_k, k, cols] for p in range(2)]
                                right = [source[:, p, k] for p in range(2)]
                            last = product(g[:, j * n:(j + 1) * n], left, right, k == 0, k == 1)
                    last.then_inc(product_made, 1)

            def unit_scores(st, b, u):
                t = unit_tile(st, u)
                if starts_tile(st, u):
                    if st.rope:
                        pe.wait_ge(sum_split, b * (2 * st.nt) + (2 * st.rotated0 + t + 1))
                    else:
                        wait_taken(st, b, ("q", t // 2))
                pe.wait_ge(keys_made, keys_when(st, b, u if st.kind == "self" else 2 * u + 1))
                pe.wait_ge(exp_made, b * st.units + (st.unit0 + u + 1))
                s = scores[u % 2]
                for qt in range(TT):
                    left = [queries[:, p, t, qt * P:(qt + 1) * P] for p in range(2)]
                    if st.kind == "self":
                        last = product(s[:, qt * N:(qt + 1) * N], left, [keys[:, u, p] for p in range(2)], True, True)
                    else:
                        last = product(s[:, qt * 2 * M:(qt + 1) * 2 * M], left,
                                       [keys[:, 2 * u:2 * u + 2, p, 0:M] for p in range(2)], True, True)
                last.then_inc(scores_made, 1)

            def unit_turn(st, b, u):
                pe.wait_ge(probs_made, b * st.units + (st.unit0 + u + 1))
                o = turned[u % 2]
                w = row_width(st)
                for i in range(2):
                    for qt in range(TT):
                        dst = slice(i * N + qt * P, i * N + (qt + 1) * P)
                        if st.kind == "self":
                            last = nc.tensor.transpose(o[:, dst], probs[:, u % 4, qt * N + i * P:qt * N + (i + 1) * P],
                                                       ident[:])
                        else:
                            r = (qt * 2 + i) * w
                            last = nc.tensor.transpose(o[0:M, dst], probs[:, u % 4, r:r + w], ident[:])
                last.then_inc(turned_made, 1)

            def unit_values(st, b, u):
                t = unit_tile(st, u)
                if u == 0:
                    wait_taken(st, b, ("v", st.values - 2))
                    wait_taken(st, b, ("v", st.values - 1))
                if starts_tile(st, u):
                    pe.wait_ge(heads_taken, b * st.nt + (st.tile0 + t + 1))
                pe.wait_ge(turned_taken, b * st.units + (st.unit0 + u + 1))
                n_keys = min(P, row_width(st))
                for i in range(2):
                    v = [values[:, p, i, u] if st.kind == "self" else values[0:M, p, 0, 2 * u + i] for p in range(2)]
                    last = product(heads_out[t % 2][:, 0:N], v,
                                   [probs_t[0:n_keys, u % 2, p, i * N:(i + 1) * N] for p in range(2)],
                                   starts_tile(st, u) and i == 0, ends_tile(st, u) and i == 1)
                if ends_tile(st, u):
                    last.then_inc(heads_made, 1)

            def project_out(st, b, pieces):
                wo = [part[3] for part in weights(st)]
                for tok, t in pieces:
                    bank = bank_of(st, ("out", tok))
                    if tok == 0:
                        pe.wait_ge(heads_taken, b * st.nt + (st.tile0 + t + 1 + RING))
                    if t == 0:
                        pe.wait_ge(product_taken[bank], used(st, b, ("out", tok)))
                    last = product(prod[bank][:, 0:D], [tall[:, p, t, tok * P:(tok + 1) * P] for p in range(2)],
                                   [wo[p][:, t] for p in range(2)], t == 0, t == st.nt - 1)
                    if t == st.nt - 1:
                        last.then_inc(product_made, 1)

            def attention(st, b):
                if st.kind == "cross":
                    pe.wait_ge(ctx_copied, b + ((st.layer * (B + 1)) + 1))
                pe.wait_ge(hidden_made, b + (st.norm0 + 1))
                projections(st, b, [p for p in st.order if p[0] not in ("v", "h", "out")])
                pieces = [(tok, t) for t in range(st.nt) for tok in range(TT)]
                for s in range(st.units + 4):
                    projections(st, b, [("v", i) for i in values_at(st, s)])
                    if s < st.units:
                        unit_scores(st, b, s)
                    if s >= 4:
                        unit_values(st, b, s - 4)
                    if 2 <= s < st.units + 2:
                        unit_turn(st, b, s - 2)
                    if s - next_at(st) in (5, 6):
                        turn_hidden(st, b, [s - next_at(st) - 5])
                    if s >= st.units:
                        ready = [p for p in pieces if (s - 6) * st.nt >= (p[1] + 1) * st.units - st.nt][:5]
                        project_out(st, b, ready)
                        pieces = pieces[len(ready):]
                project_out(st, b, pieces)

            def feed_forward(st, b):
                w = ff_weights(st)
                pe.wait_ge(hidden_made, b + (st.norm0 + 1))
                for what in st.order:
                    name, f = what
                    if name == "h":
                        turn_hidden(st, b, [f])
                    if name in ("h", "out"):
                        continue
                    bank = bank_of(st, what)
                    at = f + (FT if name == "gate" else 0)
                    pe.wait_ge(product_taken[bank], used(st, b, what))
                    for k in range(DT):
                        last = product(prod[bank][:, 0:N], [w[p][0][:, k, at * P:(at + 1) * P] for p in range(2)],
                                       [hidden[:, p, k] for p in range(2)], k == 0, k == DT - 1)
                    last.then_inc(product_made, 1)
                for tok in range(TT):
                    bank = bank_of(st, ("out", tok))
                    pe.wait_ge(product_taken[bank], used(st, b, ("out", tok)))
                    for f in range(FT):
                        if tok == 0:
                            pe.wait_ge(act_made, b * FT + (st.act0 + f + 1 + 2 * RING))
                        last = product(prod[bank][:, 0:D], [tall[:, p, f, tok * P:(tok + 1) * P] for p in range(2)],
                                       [w[p][1][:, f] for p in range(2)], f == 0, f == FT - 1)
                    last.then_inc(product_made, 1)

            pe.wait_ge(consts_in, 16 * 6)
            modulation(0, 0)
            for b in range(B):
                pe.wait_ge(cn_made, b + 1)
                pe.wait_ge(product_taken[b % 2], 1 + b // 2)
                for k in range(2):
                    last = nc.tensor.transpose(prod[b % 2][0:CP, k * M:(k + 1) * M],
                                               ctx_tok[:, b, k * CP:(k + 1) * CP], ident[0:M, 0:M])
                last.then_inc(product_made, 1)
            for layer in range(1, 4):
                modulation(layer, B + 2 * layer)
            for st in STAGES:
                turn_hidden(st, START, range(DT))
                if st.index == 0:
                    pe.wait_ge(first_split, 4)
                else:
                    splitter = [s for s in STAGES if st in s.jobs][0]
                    pe.wait_ge(chunk_split, splitter.split0 + B + 1)
                with pe.Fori(0, B) as b:
                    (feed_forward if st.kind == "ff" else attention)(st, b)

        @block.scalar
        def _(act):
            def high_hidden(st, b):
                for d in range(DT):
                    bank = bank_of(st, ("h", d)) if b is not START else d % 2
                    act.wait_ge(product_taken[bank], used(st, b, ("h", d)) + 1)
                    nc.scalar.copy(hidden[:, HI, d], hidden32[:, d]).then_inc(hidden_high, 1)

            def projections(st, b, whats):
                w = row_width(st)
                late = []

                def high_sum():
                    i = late.pop(0)
                    n = N if i < st.nt else w
                    act.wait_ge(summed, summed_when(st, b, i))
                    if i >= st.nt:
                        act.wait_ge(keys_made, tile_keys_when(st, b, i - st.nt - RING))
                    o = queries[:, HI, i] if i < st.nt else key_tile[:, i % 2, HI, 0:n]
                    nc.scalar.copy(o, sum32[:, i % 2, 0:n]).then_inc(sum_high, 1)

                for what in whats:
                    name, i = what
                    bank = bank_of(st, what)
                    g = prod[bank]
                    act.wait_ge(product_made, made(st, b, what))
                    if name == "raw":
                        n = N if i < st.nt else w
                        act.wait_ge(cos_made, cos_when(st, b, i - RING))
                        nc.scalar.copy(raw[:, i % 2, 0:n], g[:, 0:n]).then_inc(product_taken[bank], 1)
                        late.append(i)
                        if len(late) > 3:
                            high_sum()
                        continue
                    if name == "v":
                        kt, cut = i // st.value_cuts, i % st.value_cuts
                        n_keys = min(P, w)
                        last = nc.scalar.copy(value_slots(st, HI, kt, cut, n_keys),
                                              value_source(st, g[0:n_keys, 0:st.nt * P // st.value_cuts]))
                    elif name == "ctx":
                        last = nc.scalar.activation(ctx_p[:, HI, i], g[:, 0:M], ACT.Identity,
                                                    bias=col("ctx_b2", i), scale=1.0)
                    else:
                        if name == "k":
                            act.wait_ge(keys_made, tile_keys_when(st, b, st.key_tiles * (i + 1) - 1 - 4) if st.nt == 8 else keys_when(st, b, -1))
                        n = N if name == "q" else w
                        many = 2 if name == "q" else st.key_tiles
                        bias = bias_of(st, name)
                        if bias:
                            for j in range(2):
                                o = queries[:, HI, 2 * i + j] if name == "q" else key_tile[:, (2 * i + j) % 4, HI, 0:n]
                                last = nc.scalar.activation(o, g[:, j * n:(j + 1) * n], ACT.Identity,
                                                            bias=col(bias, 2 * i + j), scale=1.0)
                        else:
                            o = queries[:, HI, 2 * i:2 * i + 2] if name == "q" else \
                                key_tile[:, many * i % 4:many * i % 4 + many, HI, 0:n]
                            last = nc.scalar.copy(o, g[:, 0:many * n].rearrange("p (j n) -> p j n", j=many))
                    last.then_inc(high_made, 1)
                while late:
                    high_sum()

            def split_chunks(st, b):
                if not st.jobs:
                    return
                act.wait_ge(chunk_in, b * (16 * len(st.jobs)) + 16 * (st.chunk0 + len(st.jobs)))
                at = 0
                for job in st.jobs:
                    c = job.columns // B
                    last = nc.scalar.copy(split_weights(job)[HI][:, bass.ds(b * c, c)], staging[:, at:at + c])
                    at += c
                last.then_inc(chunk_high, 1)

            def unit_exp(st, b, u):
                act.wait_ge(max_made, b * st.units + (st.unit0 + u + 1))
                w = row_width(st)
                for r in range(n_rows(st)):
                    last = nc.scalar.activation(probs[:, u % 4, r * w:(r + 1) * w], scores[u % 2][:, r * w:(r + 1) * w],
                                                ACT.Exp, bias=neg_max[:, u % 4, r:r + 1], scale=1.0,
                                                accum_out=sums[:, u % 4, r:r + 1])
                last.then_inc(exp_made, 1)

            def high_turned(st, b, u):
                act.wait_ge(turned_made, b * st.units + (st.unit0 + u + 1))
                n = min(P, row_width(st))
                nc.scalar.copy(probs_t[0:n, u % 2, HI], turned[u % 2][0:n]).then_inc(turned_high, 1)

            def high_heads(st, b, t):
                act.wait_ge(heads_made, b * st.nt + (st.tile0 + t + 1))
                bias = bias_of(st, "v")
                if bias:
                    last = nc.scalar.activation(tall[:, HI, t], heads_out[t % 2][:, 0:N], ACT.Identity,
                                                bias=col(bias, t), scale=1.0)
                else:
                    last = nc.scalar.copy(tall[:, HI, t], heads_out[t % 2][:, 0:N])
                last.then_inc(heads_high, 1)

            def attention(st, b):
                projections(st, b, [p for p in st.order if p[0] not in ("rot", "v", "h", "out")])
                for s in range(st.units + 4):
                    projections(st, b, [("v", i) for i in values_at(st, s)])
                    if 3 <= s < st.units + 3:
                        high_turned(st, b, s - 3)
                    if s < st.units:
                        unit_exp(st, b, s)
                    if s >= 4 and ends_tile(st, s - 4):
                        high_heads(st, b, unit_tile(st, s - 4))
                    if s == st.units:
                        high_hidden(st, b)
                split_chunks(st, b)

            def feed_forward(st, b):
                func = ACT.Gelu_apprx_tanh if st.layer == 2 else ACT.Gelu
                for what in st.order:
                    name, f = what
                    if name in ("up", "h", "out"):
                        continue
                    bank = bank_of(st, what)
                    at = f + (FT if name == "gate" else 0)
                    o = gated[:, f % 2] if name == "gate" else work[:, f % 4]
                    act.wait_ge(product_made, made(st, b, what))
                    if name == "gelu":
                        act.wait_ge(act_made, b * FT + (st.act0 + f + 1))
                    nc.scalar.activation(o, prod[bank][:, 0:N], func, bias=col(f"ff_b1_{st.layer}", at),
                                         scale=1.0).then_inc(product_taken[bank], 1)
                act.wait_ge(product_made, made(st, b, st.order[-3]))
                high_hidden(st, b)
                split_chunks(st, b)

            act.sem_inc(exp_made, RING)
            act.sem_inc(cos_made, RING)
            act.wait_ge(consts_in, 16 * 6)
            nc.scalar.activation(cond[:, 1], cond[:, 0], ACT.Exp, scale=-1.0).then_inc(silu_step, 1)
            for i in range(4):
                act.wait_ge(first_w_in[i], 16)
                nc.scalar.copy(split_weights(STAGES[0])[HI][:, 2048 * i:2048 * (i + 1)], first_w[i]).then_inc(first_high, 1)
            for st in STAGES:
                high_hidden(st, START)
                nc.scalar.activation(table_warm[:], minus_half[:, 0:1], ACT.Exp if st.kind != "ff" else
                                     ACT.Gelu_apprx_tanh if st.layer == 2 else ACT.Gelu)
                with act.Fori(0, B) as b:
                    (feed_forward if st.kind == "ff" else attention)(st, b)

        @block.vector
        def _(dve):
            def tokens_stats(st, b, t):
                i = nc.vector.bn_stats(bn[:, t], x[:, bass.ds(b + 1, 1), t])
                if t == TT - 1:
                    i.then_inc(bn_made, 1)

            def tokens_mean_var(st, b):
                dve.wait_ge(bn_made, b + (st.norm0 + 2))
                nc.vector.memset(wait_carrier[:], 0.0)
                for t in range(TT):
                    last = nc.vector.bn_aggr(mv[:, t], bn[:, t])
                last.then_inc(stats_made, 1)

            def tokens_normalise(st, b, t):
                dve.wait_ge(stats_made, b + (st.norm0 + 2))
                dve.wait_ge(rstd_made, b + (st.norm0 + 2))
                i = nc.vector.tensor_scalar(xn[:, t], x[:, bass.ds(b + 1, 1), t], mv[:, t, 0:1],
                                            rstd[:, t:t + 1], ALU.subtract, ALU.mult)
                if t == TT - 1:
                    i.then_inc(xn_made, 1)

            def hidden_in_full(st, b, width_tiles):
                n = {"self": 0, "cross": 1, "ff": 2}[st.kind]
                for d in width_tiles:
                    bank = bank_of(st, ("h", d)) if b is not START else d % 2
                    dve.wait_ge(product_made, made(st, b, ("h", d)))
                    nc.vector.tensor_scalar(hidden32[:, d], prod[bank][:, 0:N],
                                            gain[:, st.layer, n, d, bass.ds(b + 1, 1)],
                                            shift[:, st.layer, n, d, bass.ds(b + 1, 1)],
                                            ALU.mult, ALU.add).then_inc(product_taken[bank], 1)

            def low(o, src, h, bias):
                if bias is None:
                    return nc.vector.tensor_tensor(o, src, h, ALU.subtract)
                return nc.vector.scalar_tensor_tensor(o, src, bias, h, ALU.add, ALU.subtract)

            def place_keys(st, b, heads):
                w = row_width(st)
                ring = RING if st.rope else 2 * RING
                for h in heads:
                    nc.vector.tensor_scalar(keys[:, h, :, 0:w], key_tile[:, h // st.hpt % ring, :, 0:w],
                                            mask(st, h % st.hpt), None, ALU.mult).then_inc(keys_made, 1)

            def heads_of(st, t):
                return range(t * st.hpt, (t + 1) * st.hpt)

            def late_keys(st, b, late):
                t = late.pop(0)
                if st.rope:
                    dve.wait_ge(sum_split, b * (2 * st.nt) + (2 * st.rotated0 + st.nt + t + 1))
                place_keys(st, b, heads_of(st, t))

            def projections(st, b, whats, late):
                w = row_width(st)
                heads_per_unit = H // st.units

                for what in whats:
                    name, i = what
                    bank = bank_of(st, what)
                    g = prod[bank]
                    if name == "raw":
                        continue
                    if name == "rot":
                        n = N if i < st.nt else w
                        dve.wait_ge(product_taken[bank_of(st, ("raw", i))], used(st, b, ("raw", i)) + 1)
                        dve.wait_ge(summed, summed_when(st, b, i - RING))
                        nc.vector.tensor_tensor(by_cos[:, i % 2, 0:n], raw[:, i % 2, 0:n], cos_t[:, 0:n],
                                                ALU.mult).then_inc(cos_made, 1)
                        dve.wait_ge(product_made, made(st, b, what))
                        nc.vector.tensor_tensor(by_sin[:, i % 2, 0:n], g[:, 0:n], sin_t[:, 0:n],
                                                ALU.mult).then_inc(product_taken[bank], 1)
                        if i >= st.nt:
                            late.append(i - st.nt)
                            if len(late) > 2:
                                late_keys(st, b, late)
                        continue
                    dve.wait_ge(high_made, high(st, b, what))
                    if name == "v":
                        kt, cut = i // st.value_cuts, i % st.value_cuts
                        n_keys = min(P, w)
                        last = low(value_slots(st, LO, kt, cut, n_keys),
                                   value_source(st, g[0:n_keys, 0:st.nt * P // st.value_cuts]),
                                   value_slots(st, HI, kt, cut, n_keys), None)
                    elif name == "ctx":
                        last = low(ctx_p[:, LO, i], g[:, 0:M], ctx_p[:, HI, i], col("ctx_b2", i))
                    else:
                        n = N if name == "q" else w
                        bias = bias_of(st, name)
                        if bias:
                            for j in range(2):
                                t = 2 * i + j
                                o = [queries[:, p, t] if name == "q" else key_tile[:, t % 4, p, 0:n] for p in range(2)]
                                last = low(o[LO], g[:, j * n:(j + 1) * n], o[HI], col(bias, t))
                        else:
                            many = 2 if name == "q" else st.key_tiles
                            o = [queries[:, p, 2 * i:2 * i + 2] if name == "q" else
                                 key_tile[:, many * i % 4:many * i % 4 + many, p, 0:n] for p in range(2)]
                            last = low(o[LO], g[:, 0:many * n].rearrange("p (j n) -> p j n", j=many), o[HI], None)
                    last.then_inc(product_taken[bank], 1)
                    if name == "k":
                        dve.wait_ge(product_taken[bank], used(st, b, what) + 1)
                        if st.nt == 2:
                            place_keys(st, b, range(2 * heads_per_unit))
                        else:
                            for t in range(st.key_tiles * i, st.key_tiles * (i + 1)):
                                if st.key_tiles * (i + 1) == st.nt:
                                    late.append(t)
                                else:
                                    place_keys(st, b, heads_of(st, t))

            def unit_max(st, b, u):
                dve.wait_ge(scores_made, b * st.units + (st.unit0 + u + 1))
                n = n_rows(st)
                s = scores[u % 2][:, 0:n * row_width(st)].rearrange("p (r w) -> p r w", r=n)
                nc.vector.tensor_reduce(neg_max[:, u % 4, 0:n], s, AXX, ALU.max, negate=True).then_inc(max_made, 1)

            def unit_recip(st, b, u):
                dve.wait_ge(exp_made, b * st.units + (st.unit0 + u + 1 + RING))
                n = n_rows(st)
                nc.vector.reciprocal(recips[:, u % 4, 0:n], sums[:, u % 4, 0:n]).then_inc(recip_made, 1)

            def low_turned(st, b, u):
                dve.wait_ge(turned_high, b * st.units + (st.unit0 + u + 1))
                n = min(P, row_width(st))
                low(probs_t[0:n, u % 2, LO], turned[u % 2][0:n], probs_t[0:n, u % 2, HI], None).then_inc(turned_taken, 1)

            def low_heads(st, b, t):
                dve.wait_ge(heads_high, b * st.nt + (st.tile0 + t + 1))
                bias = bias_of(st, "v")
                low(tall[:, LO, t], heads_out[t % 2][:, 0:N], tall[:, HI, t],
                    col(bias, t) if bias else None).then_inc(heads_taken, 1)

            def add_out(st, b):
                dve.wait_ge(bias_added, b + (st.norm0 + 1))
                for tok in range(TT):
                    what = ("out", tok)
                    bank = bank_of(st, what)
                    dve.wait_ge(product_made, made(st, b, what))
                    xs = x[:, bass.ds(b, 1), tok]
                    nc.vector.tensor_tensor(xs, prod[bank][:, 0:D].unsqueeze(1), xs, ALU.add)\
                        .then_inc(product_taken[bank], 1)

            def attention(st, b):
                late = []
                projections(st, b, [p for p in st.order if p[0] not in ("v", "h", "out")], late)
                for s in range(st.units + 4):
                    projections(st, b, [("v", i) for i in values_at(st, s)], late)
                    step = s - next_at(st)
                    if step in (0, 1):
                        tokens_stats(st, b, step)
                    if step == 2:
                        tokens_mean_var(st, b)
                    if step in (3, 4):
                        tokens_normalise(st, b, step - 3)
                    if 1 <= s <= st.units:
                        unit_recip(st, b, s - 1)
                    if s < st.units:
                        unit_max(st, b, s)
                    if late:
                        late_keys(st, b, late)
                    if st.nt == 2 and s + 2 < st.units:
                        place_keys(st, b, range((s + 2) * H // st.units, (s + 3) * H // st.units))
                    if 3 <= s < st.units + 3:
                        low_turned(st, b, s - 3)
                    if s >= 5 and ends_tile(st, s - 5):
                        low_heads(st, b, unit_tile(st, s - 5))
                    if step in (5, 6):
                        hidden_in_full(st, b, [step - 5])
                low_heads(st, b, st.nt - 1)
                add_out(st, b)

            def feed_forward(st, b):
                def low_act(f):
                    dve.wait_ge(act_high, b * FT + (st.act0 + f + 1))
                    nc.vector.tensor_tensor(tall[:, LO, f], work[:, f % 4], tall[:, HI, f],
                                            ALU.subtract).then_inc(act_made, 1)

                for what in st.order:
                    name, f = what
                    if name == "gate":
                        continue
                    if name == "h":
                        hidden_in_full(st, b, [f])
                        continue
                    if name == "out":
                        break
                    bank = bank_of(st, what)
                    if f == 0:
                        tokens_stats(st, b, 0)
                        tokens_stats(st, b, 1)
                    if f == 1:
                        tokens_mean_var(st, b)
                    if f in (2, 3):
                        tokens_normalise(st, b, f - 2)
                    if name == "up":
                        dve.wait_ge(product_made, made(st, b, what))
                        dve.wait_ge(product_taken[bank_of(st, ("gate", f))], used(st, b, ("gate", f)) + 1)
                        dve.wait_ge(act_made, b * FT + (st.act0 + f + 1))
                        nc.vector.scalar_tensor_tensor(work[:, f % 4], prod[bank][:, 0:N], col("ff_b1_1", f),
                                                       gated[:, f % 2], ALU.add, ALU.mult)\
                            .then_inc(product_taken[bank], 1)
                    dve.wait_ge(product_taken[bank], used(st, b, what) + 1)
                    nc.vector.tensor_copy(tall[:, HI, f], work[:, f % 4]).then_inc(act_high, 1)
                    if f:
                        low_act(f - 1)
                low_act(FT - 1)
                add_out(st, b)

            def modulation(layer, at):
                nm = A[f"mod_w{layer}"].shape[1] // D
                for half in range(2):
                    dve.wait_ge(product_made, at + half + 1)
                    bias = vec[:, V[f"mod_b{layer}"] + half * nm:V[f"mod_b{layer}"] + (half + 1) * nm]
                    nc.vector.tensor_tensor(mod_sb[:, layer, half * nm:(half + 1) * nm],
                                            prod[half][:, 0:nm * B].rearrange("p (j b) -> p j b", b=B),
                                            bias.unsqueeze(2).to_broadcast([P, nm, B]),
                                            ALU.add).then_inc(product_taken[half], 1)
                dve.wait_ge(product_taken[0], at // 2 + 1)
                dve.wait_ge(product_taken[1], at // 2 + 1)
                groups = {0: [(0, 1), (0, 1), (2, 3)], 1: [(0, 1), (2, 3), (4, 5)]}.get(layer, [(1, 0), (3, 2), (5, 4)])
                for n, (scale_g, shift_g) in enumerate(groups):
                    sc = mod_sb[:, layer, 2 * scale_g:2 * scale_g + 2]
                    if f"ln_w{layer}" in V:
                        c = V[f"ln_w{layer}"] + 2 * n
                        lw = vec[:, c:c + 2].unsqueeze(2).to_broadcast([P, DT, B])
                        c = V[f"ln_b{layer}"] + 2 * n
                        lb = vec[:, c:c + 2].unsqueeze(2).to_broadcast([P, DT, B])
                        nc.vector.scalar_tensor_tensor(gain[:, layer, n, :, 0:B], sc, 1.0, lw, ALU.add, ALU.mult)
                        last = nc.vector.scalar_tensor_tensor(mod_tmp[:, layer, n], sc, 1.0, lb, ALU.add, ALU.mult)
                    else:
                        nc.vector.tensor_scalar(gain[:, layer, n, :, 0:B], sc, 1.0, None, ALU.add)
                        last = nc.vector.tensor_scalar(mod_tmp[:, layer, n], sc, 0.0, None, ALU.mult)
                last.then_inc(mod_step, 1)
                dve.wait_ge(mod_step, layer + 1)
                for n, (scale_g, shift_g) in enumerate(groups):
                    sh = mod_sb[:, layer, 2 * shift_g:2 * shift_g + 2]
                    if f"ln_w{layer}" in V:
                        last = nc.vector.tensor_tensor(shift[:, layer, n, :, 0:B], mod_tmp[:, layer, n], sh, ALU.add)
                    else:
                        last = nc.vector.tensor_copy(shift[:, layer, n, :, 0:B], sh)
                last.then_inc(mod_made, 1)

            dve.wait_ge(consts_in, 16 * 6)
            dve.wait_ge(buffers_set, 1)
            dve.sem_inc(heads_taken, RING)
            dve.sem_inc(keys_made, H)
            modulation(0, 0)
            dve.wait_ge(ctx_in, 16)
            for b in range(B):
                last = nc.vector.bn_stats(cbn[:, b], ctx_tok[:, b])
            last.then_inc(cn_step, 1)
            dve.wait_ge(cn_step, 1)
            for b in range(B):
                last = nc.vector.bn_aggr(cmv[:, b], cbn[:, b])
            last.then_inc(cn_step, 1)
            dve.wait_ge(cn_step, 2)
            dve.wait_ge(cn_rstd, 2)
            for b in range(B):
                nc.vector.tensor_scalar(ctx_tok[:, b], ctx_tok[:, b], cmv[:, b, 0:1], crs[:, 1, b:b + 1],
                                        ALU.subtract, ALU.mult).then_inc(cn_made, 1)
            for b in range(B):
                dve.wait_ge(product_made, 2 + b + 1)
                nc.vector.tensor_copy(ctx_all[:, b], prod[b % 2][0:CP, 0:2 * M].rearrange("p (k m) -> p k m", k=2))\
                    .then_inc(product_taken[b % 2], 1)
            for bank in range(2):
                dve.wait_ge(product_taken[bank], 1 + B // 2)
            for k in range(2):
                last = nc.vector.tensor_scalar(ctx_all[:, 0:B, k], ctx_all[:, 0:B, k], col("ctx_ln_w", k)[0:CP],
                                               col("ctx_ln_b", k)[0:CP], ALU.mult, ALU.add)
            last.then_inc(cn_step, 1)
            for i in range(4):
                dve.wait_ge(first_high, i + 1)
                cols = slice(2048 * i, 2048 * (i + 1))
                nc.vector.tensor_tensor(split_weights(STAGES[0])[LO][:, cols], first_w[i],
                                        split_weights(STAGES[0])[HI][:, cols], ALU.subtract).then_inc(first_split, 1)
            for step in range(3):
                dve.wait_ge(silu_step, step + 1)
                if step == 0:
                    i = nc.vector.tensor_scalar(cond[:, 1], cond[:, 1], 1.0, None, ALU.add)
                elif step == 1:
                    i = nc.vector.reciprocal(cond[:, 1], cond[:, 1])
                else:
                    i = nc.vector.tensor_tensor(cond[:, 1], cond[:, 1], cond[:, 0], ALU.mult)
                i.then_inc(silu_step, 1)
            for layer in range(1, 4):
                modulation(layer, B + 2 * layer)
            dve.wait_ge(mod_made, 4)
            dve.wait_ge(x_in, 16)
            for st in STAGES:
                if st.layer == 2 and st.kind == "self":
                    dve.wait_ge(values_zeroed, 2)
                if st.index:
                    wait_stream(dve, product_taken, STAGES[st.index - 1], B - 1)
                else:
                    dve.wait_ge(values_zeroed, 1)
                for t in range(TT):
                    tokens_stats(st, START, t)
                tokens_mean_var(st, START)
                for t in range(TT):
                    tokens_normalise(st, START, t)
                hidden_in_full(st, START, range(DT))
                with dve.Fori(0, B) as b:
                    (feed_forward if st.kind == "ff" else attention)(st, b)

        @block.gpsimd
        def _(pool):
            def carry_wait(i):
                nc.gpsimd.tensor_tensor(pool_carrier[:, i:i + 1], minus_half[:, 0:1], minus_half[:, 0:1], ALU.mult)

            def tokens_rstd(st, b):
                pool.wait_ge(stats_made, b + (st.norm0 + 2))
                eps = epsilons[:, 1 if st.layer == 2 else 0]
                nc.gpsimd.tensor_tensor(var_eps[:], mv[:, :, 1], eps, ALU.add).then_inc(eps_added, 1)
                pool.wait_ge(eps_added, b + (st.norm0 + 2))
                nc.gpsimd.tensor_tensor(rstd[:], var_eps[:], minus_half[:, 0:TT], ALU.pow).then_inc(rstd_made, 1)

            def add_bias(st, b):
                pool.wait_ge(xn_made, b + (st.norm0 + 2))
                xs = x[:, bass.ds(b + 1, 1)]
                r = row(st, f"{st.kind}_ob").unsqueeze(1).unsqueeze(1).to_broadcast([P, 1, TT, D])
                nc.gpsimd.tensor_tensor(xs, xs, r, ALU.add).then_inc(bias_added, 1)

            def low_hidden(st, b):
                pool.wait_ge(hidden_high, b * DT + (DT * (st.norm0 + 2)))
                nc.gpsimd.tensor_tensor(hidden[:, LO], hidden32[:], hidden[:, HI], ALU.subtract).then_inc(hidden_made, 1)

            def rope(st, b):
                n2 = 2 * st.nt

                def low_sum(i):
                    n = N if i < st.nt else row_width(st)
                    pool.wait_ge(sum_high, b * n2 + (2 * st.rotated0 + i + 1))
                    o = [queries[:, p, i] if i < st.nt else key_tile[:, i % 2, p, 0:n] for p in range(2)]
                    nc.gpsimd.tensor_tensor(o[LO], sum32[:, i % 2, 0:n], o[HI], ALU.subtract).then_inc(sum_split, 1)

                for i in range(n2):
                    n = N if i < st.nt else row_width(st)
                    pool.wait_ge(cos_made, cos_when(st, b, i))
                    pool.wait_ge(product_taken[bank_of(st, ("rot", i))], used(st, b, ("rot", i)) + 1)
                    if i >= RING:
                        pool.wait_ge(sum_split, b * n2 + (2 * st.rotated0 + i + 1 - RING))
                    nc.gpsimd.tensor_tensor(sum32[:, i % 2, 0:n], by_cos[:, i % 2, 0:n], by_sin[:, i % 2, 0:n],
                                            ALU.add).then_inc(summed, 1)
                    if i:
                        low_sum(i - 1)
                low_sum(n2 - 1)

            def unit_normalise(st, b, u):
                pool.wait_ge(recip_made, b * st.units + (st.unit0 + u + 1))
                n = n_rows(st)
                p = probs[:, u % 4, 0:n * row_width(st)].rearrange("p (r w) -> p r w", r=n)
                nc.gpsimd.tensor_tensor(p, p, recips[:, u % 4, 0:n].unsqueeze(2).to_broadcast([P, n, row_width(st)]),
                                        ALU.mult).then_inc(probs_made, 1)

            def next_context(st, b):
                nc.gpsimd.tensor_copy(ctx_b[:, HI].unsqueeze(1), ctx_all[:, bass.ds(b + 1, 1)]).then_inc(ctx_high, 1)
                pool.wait_ge(ctx_high, b + (st.layer * (B + 1) + 2))
                carry_wait(0)
                nc.gpsimd.tensor_tensor(ctx_b[:, LO].unsqueeze(1), ctx_all[:, bass.ds(b + 1, 1)],
                                        ctx_b[:, HI].unsqueeze(1), ALU.subtract).then_inc(ctx_copied, 1)

            def split_chunks(st, b):
                if not st.jobs:
                    return
                pool.wait_ge(chunk_high, b + (st.split0 + 1))
                carry_wait(1)
                at = 0
                for job in st.jobs:
                    c = job.columns // B
                    hi, lo = [part[:, bass.ds(b * c, c)] for part in split_weights(job)]
                    last = nc.gpsimd.tensor_tensor(lo, staging[:, at:at + c], hi, ALU.subtract)
                    at += c
                last.then_inc(chunk_split, 1)

            def attention(st, b):
                if st.rope:
                    rope(st, b)
                for s in range(st.units):
                    unit_normalise(st, b, s)
                    if s == next_at(st) + 1:
                        tokens_rstd(st, b)
                low_hidden(st, b)
                if st.kind == "cross":
                    next_context(st, b)
                add_bias(st, b)
                split_chunks(st, b)

            def feed_forward(st, b):
                tokens_rstd(st, b)
                add_bias(st, b)
                low_hidden(st, b)
                split_chunks(st, b)

            pool.sem_inc(summed, RING)
            pool.sem_inc(act_made, 2 * RING)
            pool.sem_inc(chunk_split, 1)
            nc.gpsimd.memset(minus_half[:], -0.5)
            nc.gpsimd.memset(epsilons[:, 0], 1e-5)
            nc.gpsimd.memset(epsilons[:, 1], 1e-6)
            nc.gpsimd.memset(x[:, B], 0.0)
            nc.gpsimd.memset(ctx_all[:, B], 0.0)
            nc.gpsimd.memset(gain[:], 0.0)
            nc.gpsimd.memset(shift[:], 0.0).then_inc(buffers_set, 1)
            pool.wait_ge(buffers_set, 1)
            pool.wait_ge(cn_step, 2)
            nc.gpsimd.tensor_scalar(crs[:, 0], cmv[:, :, 1], 1e-5, None, ALU.add).then_inc(cn_rstd, 1)
            pool.wait_ge(cn_rstd, 1)
            nc.gpsimd.tensor_tensor(crs[:, 1], crs[:, 0], minus_half[0:M, 0:B], ALU.pow).then_inc(cn_rstd, 1)
            pool.wait_ge(first_split, 4)
            nc.gpsimd.memset(values_r[:], 0.0).then_inc(values_zeroed, 1)
            pool.wait_ge(cn_step, 3)
            for st in STAGES:
                if st.kind == "self":
                    pool.wait_ge(rows_in[st.layer % 2], 16 * (st.layer // 2 + 1))
                if st.kind == "cross":
                    if st.layer == 1:
                        pool.wait_ge(ctx_in, 32)
                    next_context(st, START)
                if st.kind == "ff" and st.layer == 1:
                    wait_stream(pool, product_taken, STAGES[st.index - 1], B - 1)
                    nc.gpsimd.memset(values_r[:], 0.0).then_inc(values_zeroed, 1)
                tokens_rstd(st, START)
                add_bias(st, START)
                low_hidden(st, START)
                with pool.Fori(0, B) as b:
                    (feed_forward if st.kind == "ff" else attention)(st, b)



def kernel(**inputs):
    import numpy as np
    import concourse.bacc as bacc
    from concourse.bass_utils import run_bass_kernel_spmd

    w = {k: np.asarray(v) for k, v in inputs.items()}
    f32 = np.float32

    def layer_w(layer, name):
        return w[f"L{layer}_xcond_{name}"]

    def columns(a):
        return np.ascontiguousarray(a.reshape(-1, P).T)

    arrays = {
        "x": w["x"],
        "ctx": np.ascontiguousarray(w["ctx_768"].transpose(1, 0, 2)),
        "ctx_t": np.ascontiguousarray(w["ctx_768"].transpose(2, 0, 1).reshape(2, CP, B, M).transpose(1, 2, 0, 3)),
        "cond_t": np.ascontiguousarray(w["cond_1024"].T.reshape(DT, P, B).transpose(1, 0, 2)),
        "ident": np.eye(P, dtype=f32),
    }
    inv = (f32(1.0) / np.power(f32(10000.0), (np.arange(0, 64, 2, dtype=f32) / f32(64)), dtype=f32)).astype(f32)
    angle = (np.arange(N, dtype=f32)[None, :] * np.repeat(inv, 2)[:, None]).astype(f32)
    angle = np.concatenate([angle, angle])
    arrays["cos_t"] = np.cos(angle).astype(f32)
    arrays["sin_t"] = np.sin(angle).astype(f32)
    rot = np.zeros((P, P), f32)
    even = np.arange(0, P, 2)
    rot[even + 1, even] = -1.0
    rot[even, even + 1] = 1.0
    arrays["rot_m"] = rot
    mask2 = np.kron(np.eye(2, dtype=f32), np.full((64, 1), 64 ** -0.5, f32))
    mask8 = np.kron(np.eye(8, dtype=f32), np.full((16, 1), 16 ** -0.5, f32))
    parts, at, vec_at = [], 0, {}

    def add(name, block):
        nonlocal at
        vec_at[name] = at
        parts.append(block)
        at += block.shape[1]

    add("mask2", mask2)
    add("mask8", mask8)
    g = layer_w
    add("mod_b0", np.concatenate([columns(g(0, n)) for n in ("g1_b", "b1_b", "g2_b", "b2_b")], 1))
    add("mod_b1", np.concatenate([columns(g(1, n)) for n in ("n1_b", "n2_b", "n3_b")], 1))
    add("mod_b2", columns(g(2, "b_ada")))
    add("mod_b3", columns(g(3, "bmod")))
    add("ln_w0", np.concatenate([columns(g(0, n)) for n in ("ln1_w", "ln1_w", "ln2_w")], 1))
    add("ln_b0", np.concatenate([columns(g(0, n)) for n in ("ln1_b", "ln1_b", "ln2_b")], 1))
    add("ln_w3", np.concatenate([columns(g(3, n)) for n in ("ln1_w", "ln2_w", "ln3_w")], 1))
    add("ln_b3", np.concatenate([columns(g(3, n)) for n in ("ln1_b", "ln2_b", "ln3_b")], 1))
    add("self_qb2", columns(g(2, "b_qkv")[0:D]))
    add("self_kb2", columns(g(2, "b_qkv")[D:2 * D]))
    add("self_qb3", columns(g(3, "bqkv")[0:D]))
    add("self_kb3", columns(g(3, "bqkv")[D:2 * D]))
    add("cross_qb3", columns(g(3, "bq")))
    add("cross_kb3", columns(g(3, "bk")))
    add("self_vb2", columns(g(2, "b_qkv")[2 * D:]))
    add("self_vb3", columns(g(3, "bqkv")[2 * D:]))
    add("cross_vb3", columns(g(3, "bv")))
    add("ctx_b2", columns(g(2, "b_ctx")))
    add("ff_b1_0", columns(g(0, "ff_b1")))
    add("ff_b1_1", columns(g(1, "ff_b1")))
    add("ff_b1_2", columns(g(2, "b_fc1")))
    add("ff_b1_3", columns(g(3, "b1")))
    for name, src in (("ctx_ln_w", "ca_lnc_w"), ("ctx_ln_b", "ca_lnc_b")):
        padded = np.zeros((P, 2), f32)
        padded[0:CP] = g(0, src).reshape(2, CP).T
        add(name, padded)
    arrays["vectors"] = np.ascontiguousarray(np.concatenate(parts, 1))
    row_at = {"self_ob": 0, "cross_ob": 1, "ff_ob": 2}
    for layer, names in enumerate((
            (g(0, "sa_bo"), g(0, "ca_bo"), g(0, "ff_b2")), (g(1, "o1_b"), g(1, "o2_b"), g(1, "ff_b2")),
            (g(2, "b_proj"), g(2, "b_out"), g(2, "b_fc2")), (g(3, "bos"), g(3, "boc"), g(3, "b2")))):
        arrays[f"rows{layer}"] = np.concatenate(names).reshape(1, -1)
    arrays["mod_w0"] = np.concatenate([g(0, n) for n in ("g1_w", "b1_w", "g2_w", "b2_w")], 1)
    arrays["mod_w1"] = np.concatenate([g(1, n) for n in ("n1_w", "n2_w", "n3_w")], 1)
    arrays["mod_w2"], arrays["mod_w3"] = g(2, "W_ada"), g(3, "Wmod")

    def chunks(a, rows_k=P):
        k, n = a.shape[0] // rows_k, a.shape[1]
        laid = np.zeros((P, k, n), f32)
        laid[0:rows_k] = a.reshape(k, rows_k, n).transpose(1, 0, 2)
        return laid.reshape(P, k * n)

    mid = 1024
    stage_parts = [
        [(g(0, "sa_wq"), P), (g(0, "sa_wkv")[:, 0:mid], P), (g(0, "sa_wkv")[:, mid:], P), (g(0, "sa_wo"), P)],
        [(g(0, "ca_wq"), P), (g(0, "ca_wkv")[:, 0:mid], CP), (g(0, "ca_wkv")[:, mid:], CP), (g(0, "ca_wo"), P)],
        [(g(0, "ff_w1"), P), (g(0, "ff_w2"), P)],
        [(g(1, "q1"), P), (g(1, "k1"), P), (g(1, "v1"), P), (g(1, "o1_w"), P)],
        [(g(1, "q2"), P), (g(1, "k2"), CP), (g(1, "v2"), CP), (g(1, "o2_w"), P)],
        [(g(1, "ff_w1"), P), (g(1, "ff_w2"), P)],
        [(g(2, "W_qkv")[:, i * D:(i + 1) * D], P) for i in range(3)] + [(g(2, "W_proj"), P)],
        [(g(2, "W_q"), P), (g(2, "W_k"), P), (g(2, "W_v"), P), (g(2, "W_out"), P), (g(2, "W_ctx"), CP)],
        [(g(2, "W_fc1"), P), (g(2, "W_fc2"), P)],
        [(g(3, "Wqkv")[:, i * D:(i + 1) * D], P) for i in range(3)] + [(g(3, "Wos"), P)],
        [(g(3, "Wq"), P), (g(3, "Wk"), CP), (g(3, "Wv"), CP), (g(3, "Woc"), P)],
        [(g(3, "W1"), P), (g(3, "W2"), P)],
    ]
    for i, matrices in enumerate(stage_parts):
        arrays[f"w{i}"] = np.concatenate([chunks(a, r) for a, r in matrices], 1)
    arrays = {k: np.ascontiguousarray(v) for k, v in arrays.items()}

    nc = bacc.Bacc("TRN2", target_bir_lowering=False, num_devices=1)
    A = {k: nc.dram_tensor(f"in_{k}", v.shape, mybir.dt.from_np(v.dtype), kind="ExternalInput").ap()
         for k, v in arrays.items()}
    A["_vec_at"], A["_row_at"] = vec_at, row_at
    out = nc.dram_tensor("out_0_dram", (B, N, D), F32, kind="ExternalOutput").ap()
    build(nc, A, out)
    r = run_bass_kernel_spmd(nc, [{f"in_{k}": v for k, v in arrays.items()}], core_ids=[0])
    return r.results[0]["out_0_dram"]
```

```python
from contextlib import ExitStack

import concourse.bass as bass
from concourse import mybir

F32 = mybir.dt.float32
F16 = mybir.dt.float16
ALU = mybir.AluOpType
ACT = mybir.ActivationFunctionType
AXX = mybir.AxisListType.X

P = 128
B = 8
N = 256
D = 256
DT = D // P
TT = N // P
H = 16
M = 77
DC = 192
CP = DC // 2
FF = 4 * D
FT = FF // P
START = -1
RING = 2
HI, LO = 0, 1


class Stage:
    pass


def plan_stages():
    stages = []
    products = 2 * 4 + B + DT
    units = tiles = rotated = pairs = key_heads = activations = splits = chunks = 0
    for layer in range(4):
        dh = 64 if layer < 2 else 16
        for kind in ("self", "cross", "ff"):
            st = Stage()
            st.index, st.layer, st.kind = len(stages), layer, kind
            st.dh, st.nt = dh, H * dh // P
            st.hpt = H // st.nt
            st.rope = layer == 0 and kind != "ff"
            st.product0, st.unit0, st.tile0, st.rotated0 = products, units, tiles, rotated
            st.norm0 = B * st.index
            if kind == "ff":
                if layer == 1:
                    order = [(w, f) for f in range(FT) for w in ("gate", "up")]
                else:
                    order = [("gelu", f) for f in range(FT)]
                st.units = 0
            else:
                order = [("ctx", t) for t in range(2)] if (layer, kind) == (2, "cross") else []
                if st.rope:
                    items = [("raw", i) for i in range(2 * st.nt)]
                    order += items[:2]
                    for i in range(2 * st.nt):
                        order += [("rot", i)] + items[i + 2:i + 3]
                elif kind == "cross" and st.nt == 8:
                    order += [("q", 0), ("k", 0), ("q", 1), ("q", 2), ("k", 1), ("q", 3)]
                else:
                    order += [(w, t) for t in range(st.nt // 2) for w in ("q", "k")]
                st.key_tiles = 4 if kind == "cross" and st.nt == 8 else 2
                st.value_cuts = 1 if st.nt == 2 and kind == "self" else 2
                st.values = (TT if kind == "self" else 1) * st.value_cuts
                st.head = order
                values, outs = [("v", c) for c in range(st.values)], [("out", t) for t in range(TT)]
                order = order + (outs + values if kind == "cross" and st.nt == 8 else values + outs)
                st.units = H if kind == "self" else H // 2
                units += B * st.units
                tiles += B * st.nt
                if st.rope:
                    rotated += B * st.nt
            turned = [("h", d) for d in range(DT)]
            if kind == "ff":
                at = len(order) * 3 // 4
                order = order[:at] + turned[:1] + order[at:at + 1] + turned[1:] + order[at + 1:]
            else:
                order += turned
            if kind == "ff":
                st.head = []
                order += [("out", t) for t in range(TT)]
            assert len(st.head) % 2 == 0
            assert len(order) % 2 == 0
            st.order = order
            st.place = {p: i for i, p in enumerate(order)}
            st.paired = [p for p in order if p[0] in ("ctx", "q", "k", "v")]
            st.pair0, st.key0, st.act0 = pairs, key_heads, activations
            pairs += B * len(st.paired)
            if kind == "ff":
                activations += B * FT
            else:
                key_heads += B * H
            products += B * len(order)
            if kind != "ff":
                products += st.place[("out", 0)] + TT
            st.columns = {"self": 3 * DT * st.nt * P + st.nt * D, "cross": 3 * DT * st.nt * P + st.nt * D,
                          "ff": (2 if layer == 1 else 1) * DT * FF + FT * D}[kind]
            if (layer, kind) == (2, "cross"):
                st.columns += 2 * D
            stages.append(st)
    for st in stages:
        ahead = [1, 2] if st.index == 0 else [2]
        st.jobs = [stages[st.index + a] for a in ahead if st.index + a < len(stages)]
        st.split0, st.chunk0 = splits, chunks
        splits += B if st.jobs else 0
        chunks += B * len(st.jobs)
    return stages


def high(st, b, what):
    return b * len(st.paired) + (st.pair0 + st.paired.index(what) + 1)


def made(st, b, what):
    if b is START:
        return 2 + B + what[1] + 1
    if what[0] == "out" and st.kind != "ff":
        return b * len(st.order) + (st.product0 + len(st.order) + st.place[what] + 1)
    return b * len(st.order) + (st.product0 + st.place[what] + 1)


def used(st, b, what):
    if b is START:
        return (2 + B + what[1]) // 2
    if what[0] == "out" and st.kind != "ff":
        return b * (len(st.order) // 2) + (st.product0 + len(st.order) + st.place[what]) // 2
    return b * (len(st.order) // 2) + (st.product0 + st.place[what]) // 2


def wait_stream(engine, product_taken, st, b):
    for tok in range(TT):
        engine.wait_ge(product_taken[bank_of(st, ("out", tok))], used(st, b, ("out", tok)) + 1)


def bank_of(st, what):
    return st.place[what] % 2


def build(nc, A, out):
    STAGES = plan_stages()
    with ExitStack() as ctx:
        def sb(name, shape):
            return ctx.enter_context(nc.sbuf_tensor(name, shape, F32))

        def psum(name, shape):
            return ctx.enter_context(nc.psum_tensor(name, shape, F32))

        def sem(name):
            return ctx.enter_context(nc.semaphore(name))

        x = sb("x", [P, B + 1, TT, D])
        weights_at = {"self": sb("self_w", [P, 8192]), "cross": sb("cross_w", [P, 8192]), "ff": sb("ff_w", [P, 6144])}
        staging = sb("staging", [P, 1536])

        def pair(region, *dims):
            names = [f"d{i}" for i in range(len(dims))]
            v = region[:].bitcast(F16) if len(region.shape) == 2 else None
            return v.rearrange(f"p (part {' '.join(names)}) -> p part {' '.join(names)}", part=2,
                               **dict(zip(names, dims)))

        keys_r, values_r = sb("keys", [P, H * N]), sb("values", [P, TT * H * P])
        tall_r = sb("tall", [P, 8 * N])
        keys = keys_r[:].bitcast(F16).rearrange("p (h part n) -> p h part n", h=H, part=2)
        values = pair(values_r, TT, H, P)
        queries_r = sb("queries", [P, 8 * N])
        queries = pair(queries_r, 8, N)
        tall = pair(tall_r, 8, N)
        hidden = pair(sb("hidden", [P, DT * N]), DT, N)
        hidden32 = sb("hidden32", [P, DT, N])
        probs = sb("probs", [P, 4, 512])
        probs_t = sb("probs_t", [P, 2 * 512])[:].bitcast(F16).rearrange("p (r part n) -> p r part n", r=2, part=2)
        key_tile = sb("key_tile", [P, 4 * N])[:].bitcast(F16).rearrange("p (r part n) -> p r part n", r=4, part=2)
        xn = sb("xn", [P, TT, D])
        ident = sb("ident", [P, P])
        cos_t = sb("cos_t", [P, N])
        sin_t = sb("sin_t", [P, N])
        rot_m = sb("rot_m", [P, P])
        raw = sb("raw", [P, 2, N])
        gated = raw
        work = sb("work", [P, 4, N])
        by_cos, by_sin = work[:, 0:2], work[:, 2:4]
        sum32 = hidden32
        ctx_all = sb("ctx_all", [CP, B + 1, 2, M])
        ctx_b = sb("ctx_b", [CP, 2 * M])[:].bitcast(F16).rearrange("p (part k m) -> p part k m", part=2, k=2)
        ctx_p = sb("ctx_p", [P, DT * M])[:].bitcast(F16).rearrange("p (part k m) -> p part k m", part=2, k=2)
        ctx_tok = probs[0:M, 0:3, :].rearrange("p a n -> p (a n)").rearrange("p (b d) -> p b d", b=B)
        NV = A["vectors"].shape[1]
        vec = sb("vec", [P, NV])
        NR = A["rows0"].shape[1]
        rows = sb("rows", [P, 2, NR])
        cond = sb("cond", [P, 2, DT, B])
        mod_sb = queries_r[:, 0:384].rearrange("p (l g b) -> p l g b", l=4, g=12)
        mod_tmp = queries_r[:, 384:576].rearrange("p (l n d b) -> p l n d b", l=4, n=3, d=DT)
        cbn = queries_r[0:M, 704:752].rearrange("p (b s) -> p b s", b=B)
        cmv = queries_r[0:M, 752:768].rearrange("p (b s) -> p b s", b=B)
        crs = queries_r[0:M, 768:784].rearrange("p (a b) -> p a b", a=2)
        gain = sb("gain", [P, 4, 3, DT, B + 1])
        shift = sb("shift", [P, 4, 3, DT, B + 1])
        mod_w = [tall_r[:, 0:2048], weights_at["ff"][:, 0:3072], weights_at["ff"][:, 3072:6144],
                 weights_at["cross"][:, 0:3072]]
        mod_w = [m.rearrange("p (k n) -> p k n", k=DT) for m in mod_w]
        first_w = [keys_r[:, 0:2048], keys_r[:, 2048:4096], values_r[:, 0:2048], values_r[:, 2048:4096]]
        bn = sb("bn", [P, TT, 6])
        wait_carrier = sb("wait_carrier", [P, 1])
        pool_carrier = sb("pool_carrier", [P, 3])
        table_warm = sb("table_warm", [P, 1])
        mv = sb("mv", [P, TT, 2])
        var_eps = sb("var_eps", [P, TT])
        rstd = sb("rstd", [P, TT])
        minus_half = sb("minus_half", [P, 8])
        epsilons = sb("epsilons", [P, 2, TT])
        neg_max = sb("neg_max", [P, 4, 4])
        sums = sb("sums", [P, 4, 4])
        recips = sb("recips", [P, 4, 4])

        scores = [psum(f"scores{i}", [P, 512]) for i in range(2)]
        turned = [psum(f"turned{i}", [P, 512]) for i in range(2)]
        heads_out = [psum(f"heads_out{i}", [P, 512]) for i in range(2)]
        prod = [psum(f"prod{i}", [P, 512]) for i in range(2)]

        consts_in = sem("consts_in")
        x_in = sem("x_in")
        mod_w_in = [sem(f"mod_w_in{i}") for i in range(4)]
        first_w_in = [sem(f"first_w_in{i}") for i in range(4)]
        first_high = sem("first_high")
        first_split = sem("first_split")
        chunk_in = sem("chunk_in")
        chunk_high = sem("chunk_high")
        chunk_split = sem("chunk_split")
        rows_in = [sem("rows_in_even"), sem("rows_in_odd")]
        ctx_in = sem("ctx_in")
        out_written = sem("out_written")
        buffers_set = sem("buffers_set")
        values_zeroed = sem("values_zeroed")
        silu_step = sem("silu_step")
        product_made = sem("product_made")
        product_taken = [sem("product_taken0"), sem("product_taken1")]
        mod_step = sem("mod_step")
        mod_made = sem("mod_made")
        cn_step = sem("cn_step")
        cn_rstd = sem("cn_rstd")
        cn_made = sem("cn_made")
        bn_made = sem("bn_made")
        stats_made = sem("stats_made")
        eps_added = sem("eps_added")
        rstd_made = sem("rstd_made")
        xn_made = sem("xn_made")
        bias_added = sem("bias_added")
        ctx_copied = sem("ctx_copied")
        high_made = sem("high_made")
        cos_made = sem("cos_made")
        summed = sem("summed")
        sum_high = sem("sum_high")
        sum_split = sem("sum_split")
        keys_made = sem("keys_made")
        hidden_high = sem("hidden_high")
        hidden_made = sem("hidden_made")
        act_high = sem("act_high")
        act_made = sem("act_made")
        turned_high = sem("turned_high")
        heads_high = sem("heads_high")
        ctx_high = sem("ctx_high")
        scores_made = sem("scores_made")
        max_made = sem("max_made")
        exp_made = sem("exp_made")
        recip_made = sem("recip_made")
        probs_made = sem("probs_made")
        turned_made = sem("turned_made")
        turned_taken = sem("turned_taken")
        heads_made = sem("heads_made")
        heads_taken = sem("heads_taken")

        V = A["_vec_at"]

        def col(name, i=0):
            return vec[:, V[name] + i:V[name] + i + 1]

        def row(st, name):
            i = A["_row_at"][name]
            return rows[:, st.layer % 2, i * D:(i + 1) * D]

        def mask(st, j):
            c = V["mask2" if st.hpt == 2 else "mask8"] + j
            return vec[:, c:c + 1]

        def bias_of(st, what):
            name = f"{st.kind}_{what}b{st.layer}"
            return name if name in V else None

        def split_weights(st):
            w = weights_at[st.kind][:].bitcast(F16)
            half = weights_at[st.kind].shape[1]
            return [w[:, 0:half], w[:, half:2 * half]]

        def weights(st):
            n, found = st.nt * P, []
            for w in split_weights(st):
                cuts = [w[:, i * DT * n:(i + 1) * DT * n].rearrange("p (k n) -> p k n", k=DT) for i in range(3)]
                at = 3 * DT * n
                o = w[:, at:at + st.nt * D].rearrange("p (t n) -> p t n", t=st.nt)
                c = w[0:CP, at + st.nt * D:at + st.nt * D + 2 * D].rearrange("p (k n) -> p k n", k=2) \
                    if (st.layer, st.kind) == (2, "cross") else None
                found.append((*cuts, o, c))
            return found

        def ff_weights(st):
            f = FF * (2 if st.layer == 1 else 1)
            return [(w[:, 0:DT * f].rearrange("p (k n) -> p k n", k=DT),
                     w[:, DT * f:DT * f + FT * D].rearrange("p (t n) -> p t n", t=FT)) for w in split_weights(st)]

        def value_slots(st, part, kt, half, rows_n):
            v = values[0:rows_n, part, kt]
            if st.value_cuts == 1 or st.hpt == 2:
                dims = [[st.hpt * P, H // st.value_cuts // st.hpt], [P + st.dh, st.hpt], [1, st.dh]]
            else:
                dims = [[P + st.dh, 8], [1, st.dh]]
            return bass.AP(tensor=v.tensor, offset=v.offset + half * 8 * P, ap=[list(v.ap[0])] + dims)

        def value_source(st, ap):
            if st.value_cuts == 1 or st.hpt == 2:
                return ap.rearrange("p (t j e) -> p t j e", j=st.hpt, e=st.dh)
            return ap.rearrange("p (j e) -> p j e", e=st.dh)

        def row_width(st):
            return N if st.kind == "self" else M

        def n_rows(st):
            return TT if st.kind == "self" else 2 * TT

        def summed_when(st, b, i):
            return b * (2 * st.nt) + (2 * st.rotated0 + RING + i + 1)

        def keys_when(st, b, h):
            return b * H + (st.key0 + H + h + 1)

        def tile_keys_when(st, b, t):
            return keys_when(st, b, (t + 1) * st.hpt - 1)

        def fill_at(st, step):
            values, outs = [("v", i) for i in range(st.values)], [("out", t) for t in range(TT)]
            if st.kind == "self" and st.nt == 8:
                steps = {1: values[:2], 2: values[2:], 3: outs[:1], 4: outs[1:]}
            elif st.kind == "self":
                steps = {1: values[:1], 2: values[1:], 3: outs}
            elif st.nt == 8:
                steps = {1: outs[:1], 2: outs[1:], 3: values}
            else:
                steps = {1: values, 2: outs[:1], 3: outs[1:]}
            return steps.get(step, [])

        def following(st, b):
            if isinstance(b, int) and b == B - 1 and st is not STAGES[-1]:
                return STAGES[st.index + 1], 0
            return st, b + 1

        def cos_when(st, b, i):
            return b * (2 * st.nt) + (2 * st.rotated0 + RING + i + 1)

        def unit_tile(st, u):
            return (u if st.kind == "self" else 2 * u) // st.hpt

        def ends_tile(st, u):
            return u == st.units - 1 or unit_tile(st, u + 1) != unit_tile(st, u)

        def starts_tile(st, u):
            return u == 0 or unit_tile(st, u - 1) != unit_tile(st, u)

        def next_steps(st):
            if st.kind == "self":
                return (4, 5), 6, (7, 8), (9, 10), 11
            return (0, 0), 1, (2, 3), (4, 5), 6

        def head_part(st, step):
            many = 2 if st.rope else 1
            at = (step - st.units) * many
            return st.head[at:] if step == st.units + 4 else st.head[at:at + many]

        def late_tiles(st):
            if st.nt == 2:
                return []
            return list(range(st.nt - 2 if st.rope else st.nt - st.key_tiles, st.nt))
        block = ctx.enter_context(nc.Block())

        @block.sync
        def _(sp):
            for name, dst in (("ident", ident), ("vectors", vec)):
                sp.dma_start(dst[:], A[name]).then_inc(consts_in, 16)
            sp.dma_start(cond[:, 0], A["cond_t"]).then_inc(consts_in, 16)
            for name, dst in (("rot_m", rot_m[:]), ("cos_t", cos_t[:]), ("sin_t", sin_t[:])):
                sp.dma_start(dst, A[name]).then_inc(consts_in, 16)
            sp.dma_start(rows[:, 0, :], A["rows0"][0].partition_broadcast(P)).then_inc(rows_in[0], 16)
            for layer in range(4):
                if layer == 1:
                    sp.dma_start(x[:, 0:B], A["x"].rearrange("b (t p) d -> p b t d", p=P)).then_inc(x_in, 16)
                    for i in range(4):
                        sp.dma_start(first_w[i], A["w0"][:, 2048 * i:2048 * (i + 1)]).then_inc(first_w_in[i], 16)
                sp.dma_start(mod_w[layer], A[f"mod_w{layer}"].rearrange("(k p) n -> p k n", p=P)).then_inc(mod_w_in[layer], 16)
                if layer == 0:
                    sp.dma_start(ctx_tok, A["ctx"]).then_inc(ctx_in, 16)
            for st in STAGES:
                layer = st.layer
                if st.kind == "ff" and layer < 3:
                    new = layer + 1
                    if new >= 2:
                        sp.wait_ge(bias_added, STAGES[3 * new - 3].norm0)
                    sp.dma_start(rows[:, new % 2, :], A[f"rows{new}"][0].partition_broadcast(P)).then_inc(rows_in[new % 2], 16)
                if (layer, st.kind) == (0, "ff"):
                    wait_stream(sp, product_taken, STAGES[1], B - 1)
                    sp.dma_start(ctx_all[:, 0:B], A["ctx_t"]).then_inc(ctx_in, 16)
                if st.jobs:
                    with sp.Fori(0, B) as b:
                        sp.wait_ge(chunk_split, b + (st.split0 + 1))
                        at = 0
                        for job in st.jobs:
                            c = job.columns // B
                            sp.dma_start(staging[:, at:at + c], A[f"w{job.index}"][:, bass.ds(b * c, c)]).then_inc(chunk_in, 16)
                            at += c
            last = STAGES[-1]
            to = out.rearrange("b (t p) d -> p b t d", p=P)
            with sp.Fori(0, B) as b:
                wait_stream(sp, product_taken, last, b)
                sp.dma_start(to[:, bass.ds(b, 1)], x[:, bass.ds(b, 1)]).then_inc(out_written, 16)
            sp.wait_ge(out_written, 16 * B)

        @block.tensor
        def _(pe):
            def turn_hidden(st, b, width_tiles):
                pe.wait_ge(xn_made, b + (st.norm0 + 2))
                for d in width_tiles:
                    bank = bank_of(st, ("h", d)) if b is not START else d % 2
                    pe.wait_ge(product_taken[bank], used(st, b, ("h", d)))
                    for t in range(TT):
                        last = nc.tensor.transpose(prod[bank][:, t * P:(t + 1) * P],
                                                   xn[:, t, d * P:(d + 1) * P], ident[:])
                    last.then_inc(product_made, 1)

            def wait_taken(st, b, what):
                if b is START:
                    pe.wait_ge(product_taken[what[1] % 2], used(st, b, what) + 1)
                else:
                    pe.wait_ge(product_taken[bank_of(st, what)], used(st, b, what) + 1)

            def product(o, left, right, start, stop):
                nc.tensor.matmul(o, left[HI], right[HI], start=start, stop=False)
                nc.tensor.matmul(o, left[HI], right[LO], start=False, stop=False)
                return nc.tensor.matmul(o, left[LO], right[HI], start=False, stop=stop)

            def modulation(layer, at):
                pe.wait_ge(mod_w_in[layer], 16)
                if layer == 2:
                    pe.wait_ge(silu_step, 4)
                nm = A[f"mod_w{layer}"].shape[1] // D
                c = cond[:, 0 if layer < 2 else 1]
                for half in range(2):
                    if at:
                        pe.wait_ge(product_taken[half], at // 2)
                    for j in range(nm):
                        g = half * nm + j
                        for k in range(DT):
                            last = nc.tensor.matmul(prod[half][:, j * B:(j + 1) * B],
                                                    mod_w[layer][:, k, g * P:(g + 1) * P], c[:, k],
                                                    start=(k == 0), stop=(k == DT - 1))
                    last.then_inc(product_made, 1)

            def projections(st, b, whats):
                w = weights(st)
                wq, wk, wv, wo, wc = [[part[i] for part in w] for i in range(5)]
                source = hidden if st.kind == "self" else ctx_p if st.layer == 2 else ctx_b
                rows_k = P if st.kind == "self" or st.layer == 2 else CP
                width = row_width(st)
                for what in whats:
                    name, i = what
                    bank = bank_of(st, what)
                    g = prod[bank]
                    if name == "k" and i == 0 and st.layer == 2 and st.kind == "cross":
                        wait_taken(st, b, ("ctx", 0))
                        wait_taken(st, b, ("ctx", 1))
                    if name == "rot":
                        wait_taken(st, b, ("raw", i))
                    pe.wait_ge(product_taken[bank], used(st, b, what))
                    if name == "rot":
                        n = N if i < st.nt else width
                        nc.tensor.matmul(g[:, 0:n], rot_m[:], raw[:, i % 2, 0:n],
                                         start=True, stop=True).then_inc(product_made, 1)
                        continue
                    is_q = name == "q" or (name == "raw" and i < st.nt)
                    if name == "v":
                        wide = st.nt * P // st.value_cuts
                        kt, cut = i // st.value_cuts, i % st.value_cuts
                        n_keys = min(P, width)
                        for k in range(2):
                            last = product(g[0:n_keys, 0:wide],
                                           [source[:, p, k, kt * P:kt * P + n_keys] for p in range(2)],
                                           [wv[p][0:rows_k, k, cut * wide:(cut + 1) * wide] for p in range(2)],
                                           k == 0, k == 1)
                        last.then_inc(product_made, 1)
                        continue
                    n = M if name == "ctx" else N if is_q else width
                    if name in ("q", "k"):
                        many = 2 if name == "q" else st.key_tiles
                        tiles = range(many * i, many * (i + 1))
                    else:
                        tiles = [i % st.nt]
                    for j, t in enumerate(tiles):
                        cols = slice(t * P, (t + 1) * P)
                        for k in range(2):
                            if name == "ctx":
                                left, right = [wc[p][:, k, cols] for p in range(2)], [ctx_b[:, p, k] for p in range(2)]
                            elif is_q:
                                left, right = [wq[p][:, k, cols] for p in range(2)], [hidden[:, p, k] for p in range(2)]
                            else:
                                left = [wk[p][0:rows_k, k, cols] for p in range(2)]
                                right = [source[:, p, k] for p in range(2)]
                            last = product(g[:, j * n:(j + 1) * n], left, right, k == 0, k == 1)
                    last.then_inc(product_made, 1)

            def unit_scores(st, b, u):
                t = unit_tile(st, u)
                if starts_tile(st, u):
                    if st.rope:
                        pe.wait_ge(sum_split, b * (2 * st.nt) + (2 * st.rotated0 + t + 1))
                    else:
                        wait_taken(st, b, ("q", t // 2))
                pe.wait_ge(keys_made, keys_when(st, b, u if st.kind == "self" else 2 * u + 1))
                pe.wait_ge(exp_made, b * st.units + (st.unit0 + u + 1))
                s = scores[u % 2]
                for qt in range(TT):
                    left = [queries[:, p, t, qt * P:(qt + 1) * P] for p in range(2)]
                    if st.kind == "self":
                        last = product(s[:, qt * N:(qt + 1) * N], left, [keys[:, u, p] for p in range(2)], True, True)
                    else:
                        last = product(s[:, qt * 2 * M:(qt + 1) * 2 * M], left,
                                       [keys[:, 2 * u:2 * u + 2, p, 0:M] for p in range(2)], True, True)
                last.then_inc(scores_made, 1)

            def unit_turn(st, b, u):
                pe.wait_ge(probs_made, b * st.units + (st.unit0 + u + 1))
                o = turned[u % 2]
                w = row_width(st)
                for i in range(2):
                    for qt in range(TT):
                        dst = slice(i * N + qt * P, i * N + (qt + 1) * P)
                        if st.kind == "self":
                            last = nc.tensor.transpose(o[:, dst], probs[:, u % 4, qt * N + i * P:qt * N + (i + 1) * P],
                                                       ident[:])
                        else:
                            r = (qt * 2 + i) * w
                            last = nc.tensor.transpose(o[0:M, dst], probs[:, u % 4, r:r + w], ident[:])
                last.then_inc(turned_made, 1)

            def unit_values(st, b, u):
                t = unit_tile(st, u)
                if u == 0:
                    wait_taken(st, b, ("v", st.values - 2))
                    wait_taken(st, b, ("v", st.values - 1))
                if starts_tile(st, u):
                    pe.wait_ge(heads_taken, b * st.nt + (st.tile0 + t + 1))
                pe.wait_ge(turned_taken, b * st.units + (st.unit0 + u + 1))
                n_keys = min(P, row_width(st))
                for i in range(2):
                    v = [values[:, p, i, u] if st.kind == "self" else values[0:M, p, 0, 2 * u + i] for p in range(2)]
                    last = product(heads_out[t % 2][:, 0:N], v,
                                   [probs_t[0:n_keys, u % 2, p, i * N:(i + 1) * N] for p in range(2)],
                                   starts_tile(st, u) and i == 0, ends_tile(st, u) and i == 1)
                if ends_tile(st, u):
                    last.then_inc(heads_made, 1)

            def project_out(st, b, token_tiles):
                wo = [part[3] for part in weights(st)]
                for tok, t in [(tok, t) for tok in token_tiles for t in range(st.nt)]:
                    bank = bank_of(st, ("out", tok))
                    if tok == 0:
                        pe.wait_ge(heads_taken, b * st.nt + (st.tile0 + t + 1 + RING))
                    if t == 0:
                        pe.wait_ge(product_taken[bank], used(st, b, ("out", tok)))
                    last = product(prod[bank][:, 0:D], [tall[:, p, t, tok * P:(tok + 1) * P] for p in range(2)],
                                   [wo[p][:, t] for p in range(2)], t == 0, t == st.nt - 1)
                    if t == st.nt - 1:
                        last.then_inc(product_made, 1)

            def wait_inputs(st, b):
                if st.kind == "cross":
                    pe.wait_ge(ctx_copied, b + ((st.layer * (B + 1)) + 1))
                pe.wait_ge(hidden_made, b + (st.norm0 + 1))

            def first_projections(st):
                wait_inputs(st, 0)
                projections(st, 0, st.head)

            def attention(st, b, first=False, last=False):
                for s in range(st.units + 4):
                    for what in fill_at(st, s):
                        if what[0] == "v":
                            projections(st, b, [what])
                        elif not first:
                            project_out(st, b - 1, [what[1]])
                        elif what[1] == TT - 1:
                            at = st.place[("out", 0)]
                            wait_taken(st, b, st.order[at - 2])
                            wait_taken(st, b, st.order[at - 1])
                            pe.sem_inc(product_made, TT)
                    if s < st.units:
                        unit_scores(st, b, s)
                    elif not last:
                        if s == st.units:
                            wait_inputs(st, b + 1)
                        projections(st, b + 1, head_part(st, s))
                    if s >= 4:
                        unit_values(st, b, s - 4)
                    if 2 <= s < st.units + 2:
                        unit_turn(st, b, s - 2)
                    if s in next_steps(st)[3]:
                        turn_hidden(st, b, [next_steps(st)[3].index(s)])
                if last:
                    wait_taken(st, b, ("h", 0))
                    wait_taken(st, b, ("h", 1))
                    pe.sem_inc(product_made, st.place[("out", 0)])
                    project_out(st, b, range(TT))
                else:
                    projections(st, b + 1, head_part(st, st.units + 4))

            def feed_forward(st, b):
                w = ff_weights(st)
                pe.wait_ge(hidden_made, b + (st.norm0 + 1))
                for what in st.order:
                    name, f = what
                    if name == "h":
                        turn_hidden(st, b, [f])
                    if name in ("h", "out"):
                        continue
                    bank = bank_of(st, what)
                    at = f + (FT if name == "gate" else 0)
                    pe.wait_ge(product_taken[bank], used(st, b, what))
                    for k in range(DT):
                        last = product(prod[bank][:, 0:N], [w[p][0][:, k, at * P:(at + 1) * P] for p in range(2)],
                                       [hidden[:, p, k] for p in range(2)], k == 0, k == DT - 1)
                    last.then_inc(product_made, 1)
                for tok in range(TT):
                    bank = bank_of(st, ("out", tok))
                    pe.wait_ge(product_taken[bank], used(st, b, ("out", tok)))
                    for f in range(FT):
                        if tok == 0:
                            pe.wait_ge(act_made, b * FT + (st.act0 + f + 1 + 2 * RING))
                        last = product(prod[bank][:, 0:D], [tall[:, p, f, tok * P:(tok + 1) * P] for p in range(2)],
                                       [w[p][1][:, f] for p in range(2)], f == 0, f == FT - 1)
                    last.then_inc(product_made, 1)

            pe.wait_ge(consts_in, 16 * 6)
            modulation(0, 0)
            for b in range(B):
                pe.wait_ge(cn_made, b + 1)
                pe.wait_ge(product_taken[b % 2], 1 + b // 2)
                for k in range(2):
                    last = nc.tensor.transpose(prod[b % 2][0:CP, k * M:(k + 1) * M],
                                               ctx_tok[:, b, k * CP:(k + 1) * CP], ident[0:M, 0:M])
                last.then_inc(product_made, 1)
            turn_hidden(STAGES[0], START, range(DT))
            for layer in range(1, 4):
                modulation(layer, B + DT + 2 * layer)
            for st in STAGES:
                if st.index == 0:
                    pe.wait_ge(first_split, 4)
                else:
                    splitter = [s for s in STAGES if st in s.jobs][0]
                    pe.wait_ge(chunk_split, splitter.split0 + B + 1)
                if st.kind == "ff":
                    with pe.Fori(0, B - 1) as b:
                        feed_forward(st, b)
                    feed_forward(st, B - 1)
                else:
                    first_projections(st)
                    attention(st, 0, first=True)
                    with pe.Fori(1, B - 1) as b:
                        attention(st, b)
                    attention(st, B - 1, last=True)

        @block.scalar
        def _(act):
            def high_hidden(st, b):
                for d in range(DT):
                    bank = bank_of(st, ("h", d)) if b is not START else d % 2
                    act.wait_ge(product_taken[bank], used(st, b, ("h", d)) + 1)
                    nc.scalar.copy(hidden[:, HI, d], hidden32[:, d]).then_inc(hidden_high, 1)

            def projections(st, b, whats, late=None):
                w = row_width(st)

                def high_sum():
                    i = late.pop(0)
                    n = N if i < st.nt else w
                    act.wait_ge(summed, summed_when(st, b, i))
                    if i >= st.nt:
                        act.wait_ge(keys_made, tile_keys_when(st, b, i - st.nt - RING))
                    o = queries[:, HI, i] if i < st.nt else key_tile[:, i % 2, HI, 0:n]
                    nc.scalar.copy(o, sum32[:, i % 2, 0:n]).then_inc(sum_high, 1)

                for what in whats:
                    name, i = what
                    if name == "rot":
                        continue
                    bank = bank_of(st, what)
                    g = prod[bank]
                    act.wait_ge(product_made, made(st, b, what))
                    if name == "raw":
                        n = N if i < st.nt else w
                        act.wait_ge(cos_made, cos_when(st, b, i - RING))
                        nc.scalar.copy(raw[:, i % 2, 0:n], g[:, 0:n]).then_inc(product_taken[bank], 1)
                        late.append(i)
                        if len(late) > 3:
                            high_sum()
                        continue
                    if name == "v":
                        kt, cut = i // st.value_cuts, i % st.value_cuts
                        n_keys = min(P, w)
                        last = nc.scalar.copy(value_slots(st, HI, kt, cut, n_keys),
                                              value_source(st, g[0:n_keys, 0:st.nt * P // st.value_cuts]))
                    elif name == "ctx":
                        last = nc.scalar.activation(ctx_p[:, HI, i], g[:, 0:M], ACT.Identity,
                                                    bias=col("ctx_b2", i), scale=1.0)
                    else:
                        if name == "k":
                            act.wait_ge(keys_made, tile_keys_when(st, b, st.key_tiles * (i + 1) - 1 - 4) if st.nt == 8 else keys_when(st, b, -1))
                        n = N if name == "q" else w
                        many = 2 if name == "q" else st.key_tiles
                        bias = bias_of(st, name)
                        if bias:
                            for j in range(2):
                                o = queries[:, HI, 2 * i + j] if name == "q" else key_tile[:, (2 * i + j) % 4, HI, 0:n]
                                last = nc.scalar.activation(o, g[:, j * n:(j + 1) * n], ACT.Identity,
                                                            bias=col(bias, 2 * i + j), scale=1.0)
                        else:
                            o = queries[:, HI, 2 * i:2 * i + 2] if name == "q" else \
                                key_tile[:, many * i % 4:many * i % 4 + many, HI, 0:n]
                            last = nc.scalar.copy(o, g[:, 0:many * n].rearrange("p (j n) -> p j n", j=many))
                    last.then_inc(high_made, 1)
                if whats and whats[-1] == st.head[-1]:
                    while late:
                        high_sum()

            def split_chunks(st, b):
                if not st.jobs:
                    return
                act.wait_ge(chunk_in, b * (16 * len(st.jobs)) + 16 * (st.chunk0 + len(st.jobs)))
                at = 0
                for job in st.jobs:
                    c = job.columns // B
                    last = nc.scalar.copy(split_weights(job)[HI][:, bass.ds(b * c, c)], staging[:, at:at + c])
                    at += c
                last.then_inc(chunk_high, 1)

            def unit_exp(st, b, u):
                act.wait_ge(max_made, b * st.units + (st.unit0 + u + 1))
                w = row_width(st)
                for r in range(n_rows(st)):
                    last = nc.scalar.activation(probs[:, u % 4, r * w:(r + 1) * w], scores[u % 2][:, r * w:(r + 1) * w],
                                                ACT.Exp, bias=neg_max[:, u % 4, r:r + 1], scale=1.0,
                                                accum_out=sums[:, u % 4, r:r + 1])
                last.then_inc(exp_made, 1)

            def high_turned(st, b, u):
                act.wait_ge(turned_made, b * st.units + (st.unit0 + u + 1))
                n = min(P, row_width(st))
                nc.scalar.copy(probs_t[0:n, u % 2, HI], turned[u % 2][0:n]).then_inc(turned_high, 1)

            def high_heads(st, b, t):
                act.wait_ge(heads_made, b * st.nt + (st.tile0 + t + 1))
                bias = bias_of(st, "v")
                if bias:
                    last = nc.scalar.activation(tall[:, HI, t], heads_out[t % 2][:, 0:N], ACT.Identity,
                                                bias=col(bias, t), scale=1.0)
                else:
                    last = nc.scalar.copy(tall[:, HI, t], heads_out[t % 2][:, 0:N])
                last.then_inc(heads_high, 1)

            def attention(st, b, first=False, last=False):
                late = []
                for s in range(st.units + 4):
                    if s == next_steps(st)[4]:
                        high_hidden(st, b)
                    if s == st.units and st.rope:
                        split_chunks(st, b)
                    projections(st, b, [p for p in fill_at(st, s) if p[0] == "v"])
                    if 3 <= s < st.units + 3:
                        high_turned(st, b, s - 3)
                    if s < st.units:
                        unit_exp(st, b, s)
                    elif not last:
                        projections(st, b + 1, head_part(st, s), late)
                    if s >= 4 and ends_tile(st, s - 4):
                        high_heads(st, b, unit_tile(st, s - 4))
                if not last:
                    projections(st, b + 1, head_part(st, st.units + 4), late)
                if not st.rope:
                    split_chunks(st, b)

            def feed_forward(st, b):
                func = ACT.Gelu_apprx_tanh if st.layer == 2 else ACT.Gelu
                for what in st.order:
                    name, f = what
                    if name in ("up", "h", "out"):
                        continue
                    bank = bank_of(st, what)
                    at = f + (FT if name == "gate" else 0)
                    o = gated[:, f % 2] if name == "gate" else work[:, f % 4]
                    act.wait_ge(product_made, made(st, b, what))
                    if name == "gelu":
                        act.wait_ge(act_made, b * FT + (st.act0 + f + 1))
                    nc.scalar.activation(o, prod[bank][:, 0:N], func, bias=col(f"ff_b1_{st.layer}", at),
                                         scale=1.0).then_inc(product_taken[bank], 1)
                act.wait_ge(product_made, made(st, b, st.order[-3]))
                high_hidden(st, b)
                split_chunks(st, b)

            act.sem_inc(exp_made, RING)
            act.sem_inc(cos_made, RING)
            act.wait_ge(consts_in, 16 * 6)
            nc.scalar.activation(cond[:, 1], cond[:, 0], ACT.Exp, scale=-1.0).then_inc(silu_step, 1)
            for st in STAGES:
                if st.index == 0:
                    high_hidden(st, START)
                    for i in range(4):
                        act.wait_ge(first_w_in[i], 16)
                        nc.scalar.copy(split_weights(STAGES[0])[HI][:, 2048 * i:2048 * (i + 1)], first_w[i]).then_inc(first_high, 1)
                    act.wait_ge(values_zeroed, 1)
                if st.layer == 2 and st.kind == "self":
                    act.wait_ge(values_zeroed, 2)
                nc.scalar.activation(table_warm[:], minus_half[:, 0:1], ACT.Exp if st.kind != "ff" else
                                     ACT.Gelu_apprx_tanh if st.layer == 2 else ACT.Gelu)
                if st.kind == "ff":
                    with act.Fori(0, B - 1) as b:
                        feed_forward(st, b)
                    feed_forward(st, B - 1)
                else:
                    projections(st, 0, st.head, [])
                    attention(st, 0, first=True)
                    with act.Fori(1, B - 1) as b:
                        attention(st, b)
                    attention(st, B - 1, last=True)

        @block.vector
        def _(dve):
            def tokens_stats(st, b, t):
                ts, slot = following(st, b)
                if ts is not st:
                    wait_stream(dve, product_taken, st, 0)
                i = nc.vector.bn_stats(bn[:, t], x[:, bass.ds(slot, 1), t])
                if t == TT - 1:
                    i.then_inc(bn_made, 1)

            def tokens_mean_var(st, b):
                dve.wait_ge(bn_made, b + (st.norm0 + 2))
                nc.vector.memset(wait_carrier[:], 0.0)
                for t in range(TT):
                    last = nc.vector.bn_aggr(mv[:, t], bn[:, t])
                last.then_inc(stats_made, 1)

            def tokens_normalise(st, b, t):
                dve.wait_ge(stats_made, b + (st.norm0 + 2))
                dve.wait_ge(rstd_made, b + (st.norm0 + 2))
                i = nc.vector.tensor_scalar(xn[:, t], x[:, bass.ds(following(st, b)[1], 1), t], mv[:, t, 0:1],
                                            rstd[:, t:t + 1], ALU.subtract, ALU.mult)
                if t == TT - 1:
                    i.then_inc(xn_made, 1)

            def hidden_in_full(st, b, width_tiles):
                ts, slot = following(st, b)
                n = {"self": 0, "cross": 1, "ff": 2}[ts.kind]
                for d in width_tiles:
                    bank = bank_of(st, ("h", d)) if b is not START else d % 2
                    dve.wait_ge(product_made, made(st, b, ("h", d)))
                    nc.vector.tensor_scalar(hidden32[:, d], prod[bank][:, 0:N],
                                            gain[:, ts.layer, n, d, bass.ds(slot, 1)],
                                            shift[:, ts.layer, n, d, bass.ds(slot, 1)],
                                            ALU.mult, ALU.add).then_inc(product_taken[bank], 1)

            def low(o, src, h, bias):
                if bias is None:
                    return nc.vector.tensor_tensor(o, src, h, ALU.subtract)
                return nc.vector.scalar_tensor_tensor(o, src, bias, h, ALU.add, ALU.subtract)

            def place_keys(st, b, heads):
                w = row_width(st)
                ring = RING if st.rope else 2 * RING
                for h in heads:
                    nc.vector.tensor_scalar(keys[:, h, :, 0:w], key_tile[:, h // st.hpt % ring, :, 0:w],
                                            mask(st, h % st.hpt), None, ALU.mult).then_inc(keys_made, 1)

            def heads_of(st, t):
                return range(t * st.hpt, (t + 1) * st.hpt)

            def late_keys(st, b, late):
                t = late.pop(0)
                if st.rope:
                    dve.wait_ge(sum_split, b * (2 * st.nt) + (2 * st.rotated0 + st.nt + t + 1))
                place_keys(st, b, heads_of(st, t))

            def projections(st, b, whats, late=None):
                w = row_width(st)
                heads_per_unit = H // st.units

                for what in whats:
                    name, i = what
                    bank = bank_of(st, what)
                    g = prod[bank]
                    if name == "raw":
                        continue
                    if name == "rot":
                        n = N if i < st.nt else w
                        dve.wait_ge(product_taken[bank_of(st, ("raw", i))], used(st, b, ("raw", i)) + 1)
                        dve.wait_ge(summed, summed_when(st, b, i - RING))
                        nc.vector.tensor_tensor(by_cos[:, i % 2, 0:n], raw[:, i % 2, 0:n], cos_t[:, 0:n],
                                                ALU.mult).then_inc(cos_made, 1)
                        dve.wait_ge(product_made, made(st, b, what))
                        nc.vector.tensor_tensor(by_sin[:, i % 2, 0:n], g[:, 0:n], sin_t[:, 0:n],
                                                ALU.mult).then_inc(product_taken[bank], 1)
                        if i >= st.nt:
                            late.append(i - st.nt)
                            if len(late) > 2:
                                late_keys(st, b, late)
                        continue
                    dve.wait_ge(high_made, high(st, b, what))
                    if name == "v":
                        kt, cut = i // st.value_cuts, i % st.value_cuts
                        n_keys = min(P, w)
                        last = low(value_slots(st, LO, kt, cut, n_keys),
                                   value_source(st, g[0:n_keys, 0:st.nt * P // st.value_cuts]),
                                   value_slots(st, HI, kt, cut, n_keys), None)
                    elif name == "ctx":
                        last = low(ctx_p[:, LO, i], g[:, 0:M], ctx_p[:, HI, i], col("ctx_b2", i))
                    else:
                        n = N if name == "q" else w
                        bias = bias_of(st, name)
                        if bias:
                            for j in range(2):
                                t = 2 * i + j
                                o = [queries[:, p, t] if name == "q" else key_tile[:, t % 4, p, 0:n] for p in range(2)]
                                last = low(o[LO], g[:, j * n:(j + 1) * n], o[HI], col(bias, t))
                        else:
                            many = 2 if name == "q" else st.key_tiles
                            o = [queries[:, p, 2 * i:2 * i + 2] if name == "q" else
                                 key_tile[:, many * i % 4:many * i % 4 + many, p, 0:n] for p in range(2)]
                            last = low(o[LO], g[:, 0:many * n].rearrange("p (j n) -> p j n", j=many), o[HI], None)
                    last.then_inc(product_taken[bank], 1)
                    if name == "k":
                        dve.wait_ge(product_taken[bank], used(st, b, what) + 1)
                        if st.nt == 2:
                            place_keys(st, b, range(2 * heads_per_unit))
                        else:
                            for t in range(st.key_tiles * i, st.key_tiles * (i + 1)):
                                if st.key_tiles * (i + 1) == st.nt:
                                    late.append(t)
                                else:
                                    place_keys(st, b, heads_of(st, t))

            def unit_max(st, b, u):
                dve.wait_ge(scores_made, b * st.units + (st.unit0 + u + 1))
                n = n_rows(st)
                s = scores[u % 2][:, 0:n * row_width(st)].rearrange("p (r w) -> p r w", r=n)
                nc.vector.tensor_reduce(neg_max[:, u % 4, 0:n], s, AXX, ALU.max, negate=True).then_inc(max_made, 1)

            def unit_recip(st, b, u):
                dve.wait_ge(exp_made, b * st.units + (st.unit0 + u + 1 + RING))
                n = n_rows(st)
                nc.vector.reciprocal(recips[:, u % 4, 0:n], sums[:, u % 4, 0:n]).then_inc(recip_made, 1)

            def low_turned(st, b, u):
                dve.wait_ge(turned_high, b * st.units + (st.unit0 + u + 1))
                n = min(P, row_width(st))
                low(probs_t[0:n, u % 2, LO], turned[u % 2][0:n], probs_t[0:n, u % 2, HI], None).then_inc(turned_taken, 1)

            def low_heads(st, b, t):
                dve.wait_ge(heads_high, b * st.nt + (st.tile0 + t + 1))
                bias = bias_of(st, "v")
                low(tall[:, LO, t], heads_out[t % 2][:, 0:N], tall[:, HI, t],
                    col(bias, t) if bias else None).then_inc(heads_taken, 1)

            def add_out(st, b, token_tiles):
                for tok in token_tiles:
                    dve.wait_ge(bias_added, b + (st.norm0 + 1))
                    what = ("out", tok)
                    bank = bank_of(st, what)
                    dve.wait_ge(product_made, made(st, b, what))
                    xs = x[:, bass.ds(b, 1), tok]
                    nc.vector.tensor_tensor(xs, prod[bank][:, 0:D].unsqueeze(1), xs, ALU.add)\
                        .then_inc(product_taken[bank], 1)

            def first_projections(st):
                late = []
                projections(st, 0, st.head, late)
                assert late == late_tiles(st)

            def attention(st, b, first=False, last=False):
                late, next_late = late_tiles(st), []
                for s in range(st.units + 4):
                    for what in fill_at(st, s):
                        if what[0] == "v":
                            projections(st, b, [what])
                        elif not first:
                            add_out(st, b - 1, [what[1]])
                        else:
                            bank = bank_of(st, what)
                            dve.wait_ge(product_taken[bank], used(st, b, st.order[st.place[what] - 2]) + 1)
                            dve.sem_inc(product_taken[bank], 1)
                    stats, mean_var, normalise, turn, _ = next_steps(st)
                    for t in range(TT):
                        if s == stats[t]:
                            tokens_stats(st, b, t)
                    if s == mean_var:
                        tokens_mean_var(st, b)
                    if s in normalise:
                        tokens_normalise(st, b, normalise.index(s))
                    if 1 <= s <= st.units:
                        unit_recip(st, b, s - 1)
                    if s < st.units:
                        unit_max(st, b, s)
                    if late:
                        late_keys(st, b, late)
                    if st.nt == 2 and s + 2 < st.units:
                        place_keys(st, b, range((s + 2) * H // st.units, (s + 3) * H // st.units))
                    if 3 <= s < st.units + 3:
                        low_turned(st, b, s - 3)
                    if s >= 5 and ends_tile(st, s - 5):
                        low_heads(st, b, unit_tile(st, s - 5))
                    if s in turn:
                        hidden_in_full(st, b, [turn.index(s)])
                    if s >= st.units and not last:
                        projections(st, b + 1, head_part(st, s), next_late)
                low_heads(st, b, st.nt - 1)
                if last:
                    for bank in range(2):
                        dve.wait_ge(product_taken[bank], used(st, b, ("h", bank)) + 1)
                        dve.sem_inc(product_taken[bank], st.place[("out", 0)] // 2)
                else:
                    projections(st, b + 1, head_part(st, st.units + 4), next_late)
                    assert next_late == late_tiles(st)
                if last:
                    add_out(st, b, range(TT))

            def feed_forward(st, b):
                def low_act(f):
                    dve.wait_ge(act_high, b * FT + (st.act0 + f + 1))
                    nc.vector.tensor_tensor(tall[:, LO, f], work[:, f % 4], tall[:, HI, f],
                                            ALU.subtract).then_inc(act_made, 1)

                for what in st.order:
                    name, f = what
                    if name == "gate":
                        continue
                    if name == "h":
                        hidden_in_full(st, b, [f])
                        continue
                    if name == "out":
                        break
                    bank = bank_of(st, what)
                    if f == 0:
                        tokens_stats(st, b, 0)
                        tokens_stats(st, b, 1)
                    if f == 1:
                        tokens_mean_var(st, b)
                    if f in (2, 3):
                        tokens_normalise(st, b, f - 2)
                    if name == "up":
                        dve.wait_ge(product_made, made(st, b, what))
                        dve.wait_ge(product_taken[bank_of(st, ("gate", f))], used(st, b, ("gate", f)) + 1)
                        dve.wait_ge(act_made, b * FT + (st.act0 + f + 1))
                        nc.vector.scalar_tensor_tensor(work[:, f % 4], prod[bank][:, 0:N], col("ff_b1_1", f),
                                                       gated[:, f % 2], ALU.add, ALU.mult)\
                            .then_inc(product_taken[bank], 1)
                    dve.wait_ge(product_taken[bank], used(st, b, what) + 1)
                    nc.vector.tensor_copy(tall[:, HI, f], work[:, f % 4]).then_inc(act_high, 1)
                    if f:
                        low_act(f - 1)
                low_act(FT - 1)
                add_out(st, b, range(TT))

            def modulation(layer, at):
                nm = A[f"mod_w{layer}"].shape[1] // D
                for half in range(2):
                    dve.wait_ge(product_made, at + half + 1)
                    bias = vec[:, V[f"mod_b{layer}"] + half * nm:V[f"mod_b{layer}"] + (half + 1) * nm]
                    nc.vector.tensor_tensor(mod_sb[:, layer, half * nm:(half + 1) * nm],
                                            prod[half][:, 0:nm * B].rearrange("p (j b) -> p j b", b=B),
                                            bias.unsqueeze(2).to_broadcast([P, nm, B]),
                                            ALU.add).then_inc(product_taken[half], 1)
                dve.wait_ge(product_taken[0], at // 2 + 1)
                dve.wait_ge(product_taken[1], at // 2 + 1)
                groups = {0: [(0, 1), (0, 1), (2, 3)], 1: [(0, 1), (2, 3), (4, 5)]}.get(layer, [(1, 0), (3, 2), (5, 4)])
                for n, (scale_g, shift_g) in enumerate(groups):
                    sc = mod_sb[:, layer, 2 * scale_g:2 * scale_g + 2]
                    if f"ln_w{layer}" in V:
                        c = V[f"ln_w{layer}"] + 2 * n
                        lw = vec[:, c:c + 2].unsqueeze(2).to_broadcast([P, DT, B])
                        c = V[f"ln_b{layer}"] + 2 * n
                        lb = vec[:, c:c + 2].unsqueeze(2).to_broadcast([P, DT, B])
                        nc.vector.scalar_tensor_tensor(gain[:, layer, n, :, 0:B], sc, 1.0, lw, ALU.add, ALU.mult)
                        last = nc.vector.scalar_tensor_tensor(mod_tmp[:, layer, n], sc, 1.0, lb, ALU.add, ALU.mult)
                    else:
                        nc.vector.tensor_scalar(gain[:, layer, n, :, 0:B], sc, 1.0, None, ALU.add)
                        last = nc.vector.tensor_scalar(mod_tmp[:, layer, n], sc, 0.0, None, ALU.mult)
                last.then_inc(mod_step, 1)
                dve.wait_ge(mod_step, layer + 1)
                for n, (scale_g, shift_g) in enumerate(groups):
                    sh = mod_sb[:, layer, 2 * shift_g:2 * shift_g + 2]
                    if f"ln_w{layer}" in V:
                        last = nc.vector.tensor_tensor(shift[:, layer, n, :, 0:B], mod_tmp[:, layer, n], sh, ALU.add)
                    else:
                        last = nc.vector.tensor_copy(shift[:, layer, n, :, 0:B], sh)
                last.then_inc(mod_made, 1)

            dve.wait_ge(consts_in, 16 * 6)
            dve.wait_ge(buffers_set, 1)
            dve.sem_inc(heads_taken, RING)
            dve.sem_inc(keys_made, H)
            modulation(0, 0)
            dve.wait_ge(ctx_in, 16)
            for b in range(B):
                last = nc.vector.bn_stats(cbn[:, b], ctx_tok[:, b])
            last.then_inc(cn_step, 1)
            dve.wait_ge(cn_step, 1)
            for b in range(B):
                last = nc.vector.bn_aggr(cmv[:, b], cbn[:, b])
            last.then_inc(cn_step, 1)
            dve.wait_ge(cn_step, 2)
            dve.wait_ge(cn_rstd, 2)
            for b in range(B):
                nc.vector.tensor_scalar(ctx_tok[:, b], ctx_tok[:, b], cmv[:, b, 0:1], crs[:, 1, b:b + 1],
                                        ALU.subtract, ALU.mult).then_inc(cn_made, 1)
            for b in range(B):
                dve.wait_ge(product_made, 2 + b + 1)
                nc.vector.tensor_copy(ctx_all[:, b], prod[b % 2][0:CP, 0:2 * M].rearrange("p (k m) -> p k m", k=2))\
                    .then_inc(product_taken[b % 2], 1)
            for bank in range(2):
                dve.wait_ge(product_taken[bank], 1 + B // 2)
            for k in range(2):
                last = nc.vector.tensor_scalar(ctx_all[:, 0:B, k], ctx_all[:, 0:B, k], col("ctx_ln_w", k)[0:CP],
                                               col("ctx_ln_b", k)[0:CP], ALU.mult, ALU.add)
            last.then_inc(cn_step, 1)
            for step in range(3):
                dve.wait_ge(silu_step, step + 1)
                if step == 0:
                    i = nc.vector.tensor_scalar(cond[:, 1], cond[:, 1], 1.0, None, ALU.add)
                elif step == 1:
                    i = nc.vector.reciprocal(cond[:, 1], cond[:, 1])
                else:
                    i = nc.vector.tensor_tensor(cond[:, 1], cond[:, 1], cond[:, 0], ALU.mult)
                i.then_inc(silu_step, 1)
            dve.wait_ge(mod_made, 1)
            dve.wait_ge(x_in, 16)
            for t in range(TT):
                tokens_stats(STAGES[0], START, t)
            tokens_mean_var(STAGES[0], START)
            for t in range(TT):
                tokens_normalise(STAGES[0], START, t)
            hidden_in_full(STAGES[0], START, range(DT))
            for i in range(4):
                dve.wait_ge(first_high, i + 1)
                cols = slice(2048 * i, 2048 * (i + 1))
                nc.vector.tensor_tensor(split_weights(STAGES[0])[LO][:, cols], first_w[i],
                                        split_weights(STAGES[0])[HI][:, cols], ALU.subtract).then_inc(first_split, 1)
                if i == 1:
                    modulation(1, B + DT + 2)
            for layer in range(2, 4):
                modulation(layer, B + DT + 2 * layer)
            dve.wait_ge(mod_made, 4)
            dve.wait_ge(values_zeroed, 1)
            for st in STAGES:
                if st.layer == 2 and st.kind == "self":
                    dve.wait_ge(values_zeroed, 2)
                if st.index:
                    wait_stream(dve, product_taken, STAGES[st.index - 1], B - 1)
                if st.kind == "ff":
                    with dve.Fori(0, B - 1) as b:
                        feed_forward(st, b)
                    feed_forward(st, B - 1)
                else:
                    first_projections(st)
                    attention(st, 0, first=True)
                    with dve.Fori(1, B - 1) as b:
                        attention(st, b)
                    attention(st, B - 1, last=True)

        @block.gpsimd
        def _(pool):
            def carry_wait(i):
                nc.gpsimd.tensor_tensor(pool_carrier[:, i:i + 1], minus_half[:, 0:1], minus_half[:, 0:1], ALU.mult)

            def tokens_rstd(st, b):
                pool.wait_ge(stats_made, b + (st.norm0 + 2))
                eps = epsilons[:, 1 if following(st, b)[0].layer == 2 else 0]
                nc.gpsimd.tensor_tensor(var_eps[:], mv[:, :, 1], eps, ALU.add).then_inc(eps_added, 1)
                pool.wait_ge(eps_added, b + (st.norm0 + 2))
                nc.gpsimd.tensor_tensor(rstd[:], var_eps[:], minus_half[:, 0:TT], ALU.pow).then_inc(rstd_made, 1)

            def add_bias(st, b):
                pool.wait_ge(xn_made, b + (st.norm0 + 2))
                ts, slot = following(st, b)
                xs = x[:, bass.ds(slot, 1)]
                r = row(ts, f"{ts.kind}_ob").unsqueeze(1).unsqueeze(1).to_broadcast([P, 1, TT, D])
                nc.gpsimd.tensor_tensor(xs, xs, r, ALU.add).then_inc(bias_added, 1)

            def low_hidden(st, b):
                pool.wait_ge(hidden_high, b * DT + (DT * (st.norm0 + 2)))
                nc.gpsimd.tensor_tensor(hidden[:, LO], hidden32[:], hidden[:, HI], ALU.subtract).then_inc(hidden_made, 1)

            def rope(st, b):
                n2 = 2 * st.nt

                def low_sum(i):
                    n = N if i < st.nt else row_width(st)
                    pool.wait_ge(sum_high, b * n2 + (2 * st.rotated0 + i + 1))
                    o = [queries[:, p, i] if i < st.nt else key_tile[:, i % 2, p, 0:n] for p in range(2)]
                    nc.gpsimd.tensor_tensor(o[LO], sum32[:, i % 2, 0:n], o[HI], ALU.subtract).then_inc(sum_split, 1)

                for i in range(n2):
                    n = N if i < st.nt else row_width(st)
                    pool.wait_ge(cos_made, cos_when(st, b, i))
                    pool.wait_ge(product_taken[bank_of(st, ("rot", i))], used(st, b, ("rot", i)) + 1)
                    if i >= RING:
                        pool.wait_ge(sum_split, b * n2 + (2 * st.rotated0 + i + 1 - RING))
                    nc.gpsimd.tensor_tensor(sum32[:, i % 2, 0:n], by_cos[:, i % 2, 0:n], by_sin[:, i % 2, 0:n],
                                            ALU.add).then_inc(summed, 1)
                    if i:
                        low_sum(i - 1)
                low_sum(n2 - 1)

            def unit_normalise(st, b, u):
                pool.wait_ge(recip_made, b * st.units + (st.unit0 + u + 1))
                n = n_rows(st)
                p = probs[:, u % 4, 0:n * row_width(st)].rearrange("p (r w) -> p r w", r=n)
                nc.gpsimd.tensor_tensor(p, p, recips[:, u % 4, 0:n].unsqueeze(2).to_broadcast([P, n, row_width(st)]),
                                        ALU.mult).then_inc(probs_made, 1)

            def next_context(st, b):
                nc.gpsimd.tensor_copy(ctx_b[:, HI].unsqueeze(1), ctx_all[:, bass.ds(b + 1, 1)]).then_inc(ctx_high, 1)
                pool.wait_ge(ctx_high, b + (st.layer * (B + 1) + 2))
                carry_wait(0)
                nc.gpsimd.tensor_tensor(ctx_b[:, LO].unsqueeze(1), ctx_all[:, bass.ds(b + 1, 1)],
                                        ctx_b[:, HI].unsqueeze(1), ALU.subtract).then_inc(ctx_copied, 1)

            def split_chunks(st, b):
                if not st.jobs:
                    return
                pool.wait_ge(chunk_high, b + (st.split0 + 1))
                carry_wait(1)
                at = 0
                for job in st.jobs:
                    c = job.columns // B
                    hi, lo = [part[:, bass.ds(b * c, c)] for part in split_weights(job)]
                    last = nc.gpsimd.tensor_tensor(lo, staging[:, at:at + c], hi, ALU.subtract)
                    at += c
                last.then_inc(chunk_split, 1)

            def attention(st, b, first=False, last=False):
                for s in range(st.units):
                    if s == next_steps(st)[1]:
                        tokens_rstd(st, b)
                    if s == next_steps(st)[4]:
                        low_hidden(st, b)
                    unit_normalise(st, b, s)
                    if s == 5 and st.kind == "cross":
                        next_context(st, b)
                    if s == st.units - 2 and st.rope:
                        add_bias(st, b)
                if st.rope:
                    split_chunks(st, b)
                    if not last:
                        rope(st, b + 1)
                else:
                    add_bias(st, b)
                    split_chunks(st, b)

            def feed_forward(st, b):
                tokens_rstd(st, b)
                add_bias(st, b)
                low_hidden(st, b)
                split_chunks(st, b)

            pool.sem_inc(summed, RING)
            pool.sem_inc(act_made, 2 * RING)
            pool.sem_inc(chunk_split, 1)
            nc.gpsimd.memset(minus_half[:], -0.5)
            nc.gpsimd.memset(epsilons[:, 0], 1e-5)
            nc.gpsimd.memset(epsilons[:, 1], 1e-6)
            nc.gpsimd.memset(x[:, B], 0.0)
            nc.gpsimd.memset(ctx_all[:, B], 0.0)
            nc.gpsimd.memset(gain[:], 0.0)
            nc.gpsimd.memset(shift[:], 0.0).then_inc(buffers_set, 1)
            pool.wait_ge(buffers_set, 1)
            pool.wait_ge(cn_step, 2)
            nc.gpsimd.tensor_scalar(crs[:, 0], cmv[:, :, 1], 1e-5, None, ALU.add).then_inc(cn_rstd, 1)
            pool.wait_ge(cn_rstd, 1)
            nc.gpsimd.tensor_tensor(crs[:, 1], crs[:, 0], minus_half[0:M, 0:B], ALU.pow).then_inc(cn_rstd, 1)
            pool.wait_ge(cn_step, 3)
            for st in STAGES:
                if st.index == 0:
                    pool.wait_ge(rows_in[0], 16)
                if st.kind == "cross":
                    if st.layer == 1:
                        pool.wait_ge(ctx_in, 32)
                    next_context(st, START)
                if st.kind == "ff" and st.layer == 1:
                    wait_stream(pool, product_taken, STAGES[st.index - 1], B - 1)
                    nc.gpsimd.memset(values_r[:], 0.0).then_inc(values_zeroed, 1)
                if st.index == 0:
                    tokens_rstd(st, START)
                    add_bias(st, START)
                    low_hidden(st, START)
                    pool.wait_ge(first_split, 4)
                    nc.gpsimd.memset(values_r[:], 0.0).then_inc(values_zeroed, 1)
                if st.kind == "ff":
                    with pool.Fori(0, B - 1) as b:
                        feed_forward(st, b)
                    if st.layer < 3:
                        pool.wait_ge(rows_in[(st.layer + 1) % 2], 16 * ((st.layer + 1) // 2 + 1))
                    feed_forward(st, B - 1)
                else:
                    if st.rope:
                        rope(st, 0)
                    attention(st, 0, first=True)
                    with pool.Fori(1, B - 1) as b:
                        attention(st, b)
                    attention(st, B - 1, last=True)



def kernel(**inputs):
    import numpy as np
    import concourse.bacc as bacc
    from concourse.bass_utils import run_bass_kernel_spmd

    w = {k: np.asarray(v) for k, v in inputs.items()}
    f32 = np.float32

    def layer_w(layer, name):
        return w[f"L{layer}_xcond_{name}"]

    def columns(a):
        return np.ascontiguousarray(a.reshape(-1, P).T)

    arrays = {
        "x": w["x"],
        "ctx": np.ascontiguousarray(w["ctx_768"].transpose(1, 0, 2)),
        "ctx_t": np.ascontiguousarray(w["ctx_768"].transpose(2, 0, 1).reshape(2, CP, B, M).transpose(1, 2, 0, 3)),
        "cond_t": np.ascontiguousarray(w["cond_1024"].T.reshape(DT, P, B).transpose(1, 0, 2)),
        "ident": np.eye(P, dtype=f32),
    }
    inv = (f32(1.0) / np.power(f32(10000.0), (np.arange(0, 64, 2, dtype=f32) / f32(64)), dtype=f32)).astype(f32)
    angle = (np.arange(N, dtype=f32)[None, :] * np.repeat(inv, 2)[:, None]).astype(f32)
    angle = np.concatenate([angle, angle])
    arrays["cos_t"] = np.cos(angle).astype(f32)
    arrays["sin_t"] = np.sin(angle).astype(f32)
    rot = np.zeros((P, P), f32)
    even = np.arange(0, P, 2)
    rot[even + 1, even] = -1.0
    rot[even, even + 1] = 1.0
    arrays["rot_m"] = rot
    mask2 = np.kron(np.eye(2, dtype=f32), np.full((64, 1), 64 ** -0.5, f32))
    mask8 = np.kron(np.eye(8, dtype=f32), np.full((16, 1), 16 ** -0.5, f32))
    parts, at, vec_at = [], 0, {}

    def add(name, block):
        nonlocal at
        vec_at[name] = at
        parts.append(block)
        at += block.shape[1]

    add("mask2", mask2)
    add("mask8", mask8)
    g = layer_w
    add("mod_b0", np.concatenate([columns(g(0, n)) for n in ("g1_b", "b1_b", "g2_b", "b2_b")], 1))
    add("mod_b1", np.concatenate([columns(g(1, n)) for n in ("n1_b", "n2_b", "n3_b")], 1))
    add("mod_b2", columns(g(2, "b_ada")))
    add("mod_b3", columns(g(3, "bmod")))
    add("ln_w0", np.concatenate([columns(g(0, n)) for n in ("ln1_w", "ln1_w", "ln2_w")], 1))
    add("ln_b0", np.concatenate([columns(g(0, n)) for n in ("ln1_b", "ln1_b", "ln2_b")], 1))
    add("ln_w3", np.concatenate([columns(g(3, n)) for n in ("ln1_w", "ln2_w", "ln3_w")], 1))
    add("ln_b3", np.concatenate([columns(g(3, n)) for n in ("ln1_b", "ln2_b", "ln3_b")], 1))
    add("self_qb2", columns(g(2, "b_qkv")[0:D]))
    add("self_kb2", columns(g(2, "b_qkv")[D:2 * D]))
    add("self_qb3", columns(g(3, "bqkv")[0:D]))
    add("self_kb3", columns(g(3, "bqkv")[D:2 * D]))
    add("cross_qb3", columns(g(3, "bq")))
    add("cross_kb3", columns(g(3, "bk")))
    add("self_vb2", columns(g(2, "b_qkv")[2 * D:]))
    add("self_vb3", columns(g(3, "bqkv")[2 * D:]))
    add("cross_vb3", columns(g(3, "bv")))
    add("ctx_b2", columns(g(2, "b_ctx")))
    add("ff_b1_0", columns(g(0, "ff_b1")))
    add("ff_b1_1", columns(g(1, "ff_b1")))
    add("ff_b1_2", columns(g(2, "b_fc1")))
    add("ff_b1_3", columns(g(3, "b1")))
    for name, src in (("ctx_ln_w", "ca_lnc_w"), ("ctx_ln_b", "ca_lnc_b")):
        padded = np.zeros((P, 2), f32)
        padded[0:CP] = g(0, src).reshape(2, CP).T
        add(name, padded)
    arrays["vectors"] = np.ascontiguousarray(np.concatenate(parts, 1))
    row_at = {"self_ob": 0, "cross_ob": 1, "ff_ob": 2}
    for layer, names in enumerate((
            (g(0, "sa_bo"), g(0, "ca_bo"), g(0, "ff_b2")), (g(1, "o1_b"), g(1, "o2_b"), g(1, "ff_b2")),
            (g(2, "b_proj"), g(2, "b_out"), g(2, "b_fc2")), (g(3, "bos"), g(3, "boc"), g(3, "b2")))):
        arrays[f"rows{layer}"] = np.concatenate(names).reshape(1, -1)
    arrays["mod_w0"] = np.concatenate([g(0, n) for n in ("g1_w", "b1_w", "g2_w", "b2_w")], 1)
    arrays["mod_w1"] = np.concatenate([g(1, n) for n in ("n1_w", "n2_w", "n3_w")], 1)
    arrays["mod_w2"], arrays["mod_w3"] = g(2, "W_ada"), g(3, "Wmod")

    def chunks(a, rows_k=P):
        k, n = a.shape[0] // rows_k, a.shape[1]
        laid = np.zeros((P, k, n), f32)
        laid[0:rows_k] = a.reshape(k, rows_k, n).transpose(1, 0, 2)
        return laid.reshape(P, k * n)

    mid = 1024
    stage_parts = [
        [(g(0, "sa_wq"), P), (g(0, "sa_wkv")[:, 0:mid], P), (g(0, "sa_wkv")[:, mid:], P), (g(0, "sa_wo"), P)],
        [(g(0, "ca_wq"), P), (g(0, "ca_wkv")[:, 0:mid], CP), (g(0, "ca_wkv")[:, mid:], CP), (g(0, "ca_wo"), P)],
        [(g(0, "ff_w1"), P), (g(0, "ff_w2"), P)],
        [(g(1, "q1"), P), (g(1, "k1"), P), (g(1, "v1"), P), (g(1, "o1_w"), P)],
        [(g(1, "q2"), P), (g(1, "k2"), CP), (g(1, "v2"), CP), (g(1, "o2_w"), P)],
        [(g(1, "ff_w1"), P), (g(1, "ff_w2"), P)],
        [(g(2, "W_qkv")[:, i * D:(i + 1) * D], P) for i in range(3)] + [(g(2, "W_proj"), P)],
        [(g(2, "W_q"), P), (g(2, "W_k"), P), (g(2, "W_v"), P), (g(2, "W_out"), P), (g(2, "W_ctx"), CP)],
        [(g(2, "W_fc1"), P), (g(2, "W_fc2"), P)],
        [(g(3, "Wqkv")[:, i * D:(i + 1) * D], P) for i in range(3)] + [(g(3, "Wos"), P)],
        [(g(3, "Wq"), P), (g(3, "Wk"), CP), (g(3, "Wv"), CP), (g(3, "Woc"), P)],
        [(g(3, "W1"), P), (g(3, "W2"), P)],
    ]
    for i, matrices in enumerate(stage_parts):
        arrays[f"w{i}"] = np.concatenate([chunks(a, r) for a, r in matrices], 1)
    arrays = {k: np.ascontiguousarray(v) for k, v in arrays.items()}

    nc = bacc.Bacc("TRN2", target_bir_lowering=False, num_devices=1)
    A = {k: nc.dram_tensor(f"in_{k}", v.shape, mybir.dt.from_np(v.dtype), kind="ExternalInput").ap()
         for k, v in arrays.items()}
    A["_vec_at"], A["_row_at"] = vec_at, row_at
    out = nc.dram_tensor("out_0_dram", (B, N, D), F32, kind="ExternalOutput").ap()
    build(nc, A, out)
    r = run_bass_kernel_spmd(nc, [{f"in_{k}": v for k, v in arrays.items()}], core_ids=[0])
    return r.results[0]["out_0_dram"]
```
